# Optimizing a Trainium2 kernel written in Bass

```python
import numpy as np
import jax
import jax.numpy as jnp

def _softmax(x, axis=-1):
    return jax.nn.softmax(x, axis=axis)

def _gelu(x):
    return jax.nn.gelu(x, approximate=True)

def _silu(x):
    return jax.nn.silu(x)

def _sigmoid(x):
    return jax.nn.sigmoid(x)

def _layernorm(x, axis=-1, eps=1e-05):
    m = jnp.mean(x, axis=axis, keepdims=True)
    v = jnp.var(x, axis=axis, keepdims=True)
    return (x - m) / jnp.sqrt(v + eps)

def _scatter_add(tgt, idx, src, axis=0):
    return tgt.at[idx].add(src)

def _segment_sum(src, seg, n):
    return jax.ops.segment_sum(src, seg, n)
kernel_name = 'mk_xattn_ffn_d1_seqx_r8_473591'

def setup_inputs(seed: int=0):
    np.random.seed(seed)
    _w = jnp.asarray

    def _rec_inputs():
        import jax
        import jax.numpy as jnp
        _rk = jax.random.key(seed)
        x = -0.0002928 + 1 * jax.random.normal(jax.random.fold_in(_rk, 1), (32, 64, 128), jnp.float32)
        _lenS = 64 - jax.random.randint(jax.random.fold_in(_rk, 7), (32,), 0, max(1, 64 // 4) + 1, jnp.int32)
        _lenS2 = 64 - jax.random.randint(jax.random.fold_in(_rk, 8), (32,), 0, max(1, 64 // 4) + 1, jnp.int32)
        _ctx_1024P = jax.random.normal(jax.random.fold_in(_rk, 11), (32, 16, 128), jnp.float32)
        _ctx_1024c = jax.random.dirichlet(jax.random.fold_in(_rk, 511), 0.3 * jnp.ones((16,), jnp.float32), (32, 64))
        _ctx_1024t = jnp.einsum('bsk,bkd->bsd', _ctx_1024c, _ctx_1024P)
        _ctx_1024t = _ctx_1024t * jax.lax.rsqrt(jnp.mean(jnp.square(_ctx_1024t)) + 1e-12) * 0.953939
        ctx_1024 = -1.39393e-06 + 0.999914 * (_ctx_1024t + 0.3 * jax.random.normal(jax.random.fold_in(_rk, 611), (32, 64, 128), jnp.float32))
        _validS = jnp.arange(64)[None, :] < _lenS[:, None]
        _validS2 = jnp.arange(64)[None, :] < _lenS2[:, None]
        _causal = jnp.tril(jnp.ones((64, 64), dtype=bool))
        mask_Bx1x1xS2_bk0 = jnp.logical_not(jnp.broadcast_to(_validS2[:, None, None, :], (32, 1, 1, 64)))
        return (x, ctx_1024, mask_Bx1x1xS2_bk0)
    x, ctx_1024, mask_Bx1x1xS2_bk0 = _rec_inputs()

    def _L0_xattn_setup():
        import jax, jax.numpy as jnp
        import numpy as np
        N_HEAD = 16
        NEG_INF = -1000000000.0
        key = jax.random.key(seed)
        ks = jax.random.split(key, 8)
        B, S, D = (2, 256, 128)
        q = jax.random.normal(ks[0], (B, S, D), dtype=jnp.float32)
        k = jax.random.normal(ks[1], (B, S, D), dtype=jnp.float32)
        v = jax.random.normal(ks[2], (B, S, D), dtype=jnp.float32)
        mask = jax.random.randint(ks[3], (B, 1, 1, S), 0, 2).astype(bool)
        init = (1.0 / np.sqrt(D)).astype(np.float32) if isinstance(np.sqrt(D), np.ndarray) else np.float32(1.0 / np.sqrt(D))
        Wq = jax.random.normal(ks[4], (D, D), dtype=jnp.float32) * init
        Wk = jax.random.normal(ks[5], (D, D), dtype=jnp.float32) * init
        Wv = jax.random.normal(ks[6], (D, D), dtype=jnp.float32) * init
        Wo = jax.random.normal(ks[7], (D, D), dtype=jnp.float32) * init
        return {'q': q, 'k': k, 'v': v, 'mask': mask, 'Wq': Wq, 'Wk': Wk, 'Wv': Wv, 'Wo': Wo}
    _L0_xattn_all = _L0_xattn_setup()
    _L0_xattn_in = {k: v for k, v in _L0_xattn_all.items() if k in ('Wq', 'Wk', 'Wv', 'Wo')}
    del _L0_xattn_all

    def _L0_ffn_setup():
        import jax, jax.numpy as jnp
        import numpy as np
        DIM = 128
        EXPERT_DIM = 64
        N_EXPERTS = 16
        TOPK = 2
        SHARED_HIDDEN = EXPERT_DIM * TOPK
        B, T = (4, 128)

        def _moe_forward(x, router_w, router_bias, up_proj, gate_proj, down_proj, sh_gate, sh_up, sh_down):
            Bb, Tt, D = x.shape
            flat = x.reshape(Bb * Tt, D)
            N = flat.shape[0]
            logits = flat @ router_w.T
            topk_scores, topk_idx = jax.lax.top_k(logits + router_bias, TOPK)
            topk_scores = jax.nn.softmax(topk_scores, axis=-1)
            combine = jnp.zeros((N, N_EXPERTS), flat.dtype)
            combine = combine.at[jnp.arange(N)[:, None], topk_idx].add(topk_scores)
            up_all = jnp.einsum('nd,kde->nke', flat, up_proj)
            gate_all = jnp.einsum('nd,kde->nke', flat, gate_proj)
            hidden = jax.nn.silu(gate_all) * up_all
            down_all = jnp.einsum('nke,ked->nkd', hidden, down_proj)
            out = jnp.einsum('nk,nkd->nd', combine, down_all)
            sh_hidden = jax.nn.silu(flat @ sh_gate.T) * (flat @ sh_up.T)
            out = out + sh_hidden @ sh_down.T
            return out.reshape(Bb, Tt, D)
        key = jax.random.key(seed)
        ks = jax.random.split(key, 9)
        std = 0.02
        return {'x': jax.random.normal(ks[0], (B, T, DIM), jnp.float32), 'router_w': jax.random.normal(ks[1], (N_EXPERTS, DIM), jnp.float32) * std, 'router_bias': jnp.zeros((N_EXPERTS,), jnp.float32), 'up_proj': jax.random.normal(ks[2], (N_EXPERTS, DIM, EXPERT_DIM), jnp.float32) * std, 'gate_proj': jax.random.normal(ks[3], (N_EXPERTS, DIM, EXPERT_DIM), jnp.float32) * std, 'down_proj': jax.random.normal(ks[4], (N_EXPERTS, EXPERT_DIM, DIM), jnp.float32) * std, 'sh_gate': jax.random.normal(ks[5], (SHARED_HIDDEN, DIM), jnp.float32) * std, 'sh_up': jax.random.normal(ks[6], (SHARED_HIDDEN, DIM), jnp.float32) * std, 'sh_down': jax.random.normal(ks[7], (DIM, SHARED_HIDDEN), jnp.float32) * std}
    _L0_ffn_all = _L0_ffn_setup()
    _L0_ffn_in = {k: v for k, v in _L0_ffn_all.items() if k in ('router_w', 'router_bias', 'up_proj', 'gate_proj', 'down_proj', 'sh_gate', 'sh_up', 'sh_down')}
    del _L0_ffn_all
    return {'x': x, 'ctx_1024': ctx_1024, 'mask_Bx1x1xS2_bk0': mask_Bx1x1xS2_bk0, 'L0_xattn_Wq': _L0_xattn_in['Wq'], 'L0_xattn_Wk': _L0_xattn_in['Wk'], 'L0_xattn_Wv': _L0_xattn_in['Wv'], 'L0_xattn_Wo': _L0_xattn_in['Wo'], 'L0_ffn_router_w': _L0_ffn_in['router_w'], 'L0_ffn_router_bias': _L0_ffn_in['router_bias'], 'L0_ffn_up_proj': _L0_ffn_in['up_proj'], 'L0_ffn_gate_proj': _L0_ffn_in['gate_proj'], 'L0_ffn_down_proj': _L0_ffn_in['down_proj'], 'L0_ffn_sh_gate': _L0_ffn_in['sh_gate'], 'L0_ffn_sh_up': _L0_ffn_in['sh_up'], 'L0_ffn_sh_down': _L0_ffn_in['sh_down']}

def reference(x, ctx_1024, mask_Bx1x1xS2_bk0, L0_xattn_Wq, L0_xattn_Wk, L0_xattn_Wv, L0_xattn_Wo, L0_ffn_router_w, L0_ffn_router_bias, L0_ffn_up_proj, L0_ffn_gate_proj, L0_ffn_down_proj, L0_ffn_sh_gate, L0_ffn_sh_up, L0_ffn_sh_down):
    import jax
    import jax.numpy as jnp

    def _L0_xattn_ref(q, k, v, mask, Wq, Wk, Wv, Wo):
        import jax, jax.numpy as jnp
        import numpy as np
        N_HEAD = 16
        NEG_INF = -1000000000.0
        B, S, D = q.shape
        dk = D // N_HEAD
        scale = dk ** (-0.5)

        def split_heads(x, W):
            return (x @ W.T).reshape(B, -1, N_HEAD, dk).transpose(0, 2, 1, 3)
        qh = split_heads(q, Wq)
        kh = split_heads(k, Wk)
        vh = split_heads(v, Wv)
        scores = jnp.einsum('bhqd,bhkd->bhqk', qh, kh) / scale
        scores = jnp.where(mask, NEG_INF, scores)
        attn = jax.nn.softmax(scores, axis=-1)
        ctx = jnp.einsum('bhqk,bhkd->bhqd', attn, vh)
        ctx = ctx.transpose(0, 2, 1, 3).reshape(B, S, D)
        return ctx @ Wo.T

    def _L0_ffn_ref(x, router_w, router_bias, up_proj, gate_proj, down_proj, sh_gate, sh_up, sh_down):
        import jax, jax.numpy as jnp
        import numpy as np
        DIM = 128
        EXPERT_DIM = 64
        N_EXPERTS = 16
        TOPK = 2
        SHARED_HIDDEN = EXPERT_DIM * TOPK
        B, T = (4, 128)

        def _moe_forward(x, router_w, router_bias, up_proj, gate_proj, down_proj, sh_gate, sh_up, sh_down):
            Bb, Tt, D = x.shape
            flat = x.reshape(Bb * Tt, D)
            N = flat.shape[0]
            logits = flat @ router_w.T
            topk_scores, topk_idx = jax.lax.top_k(logits + router_bias, TOPK)
            topk_scores = jax.nn.softmax(topk_scores, axis=-1)
            combine = jnp.zeros((N, N_EXPERTS), flat.dtype)
            combine = combine.at[jnp.arange(N)[:, None], topk_idx].add(topk_scores)
            up_all = jnp.einsum('nd,kde->nke', flat, up_proj)
            gate_all = jnp.einsum('nd,kde->nke', flat, gate_proj)
            hidden = jax.nn.silu(gate_all) * up_all
            down_all = jnp.einsum('nke,ked->nkd', hidden, down_proj)
            out = jnp.einsum('nk,nkd->nd', combine, down_all)
            sh_hidden = jax.nn.silu(flat @ sh_gate.T) * (flat @ sh_up.T)
            out = out + sh_hidden @ sh_down.T
            return out.reshape(Bb, Tt, D)
        return _moe_forward(x, router_w, router_bias, up_proj, gate_proj, down_proj, sh_gate, sh_up, sh_down)
    x = x + _L0_xattn_ref(_layernorm(x, axis=-1), ctx_1024, ctx_1024, mask_Bx1x1xS2_bk0, L0_xattn_Wq, L0_xattn_Wk, L0_xattn_Wv, L0_xattn_Wo)
    x = x + _L0_ffn_ref(_layernorm(x, axis=-1), L0_ffn_router_w, L0_ffn_router_bias, L0_ffn_up_proj, L0_ffn_gate_proj, L0_ffn_down_proj, L0_ffn_sh_gate, L0_ffn_sh_up, L0_ffn_sh_down)
    return x

_drawn_inputs = setup_inputs


def setup_inputs(seed=0):
    import zlib

    import numpy as np

    out = dict(_drawn_inputs(seed))
    spreads = {'L0_ffn_router_bias': (0.0, 0.8)}
    factors = {'L0_ffn_router_w': 8.0,
     'L0_ffn_up_proj': 8.0,
     'L0_ffn_gate_proj': 8.0,
     'L0_ffn_down_proj': 8.0,
     'L0_ffn_sh_gate': 8.0,
     'L0_ffn_sh_up': 8.0,
     'L0_ffn_sh_down': 8.0}
    for name, (base, spread) in spreads.items():
        noise = np.random.default_rng([zlib.crc32(name.encode()), seed]).standard_normal(out[name].shape)
        drawn = base * np.exp(spread * noise) if base else spread * noise
        out[name] = jnp.asarray(drawn.astype(out[name].dtype))
    for name, factor in factors.items():
        out[name] = (out[name] * factor).astype(out[name].dtype)
    return out
```

```python
from contextlib import ExitStack

import numpy as np

import concourse.bass as bass
from concourse import mybir

F32 = mybir.dt.float32
BF16 = mybir.dt.bfloat16
U8 = mybir.dt.uint8
U32 = mybir.dt.uint32
ALU = mybir.AluOpType
ACT = mybir.ActivationFunctionType
AX_X = mybir.AxisListType.X

P = 128
BATCHES, S, D = 32, 64, 128
HEADS, DK = 16, 8
TOKENS = BATCHES * S
TILES = TOKENS // P
BPT = P // S
HG = HEADS // 2
ROWS = HG * DK
PAIRS = HEADS // 2
DV = DK + 1
EXPERTS, E_DIM = 16, 64
EPAIRS = EXPERTS // 2
UNITS = EPAIRS + 1
GT = 4
GROUPS = TILES // GT
GN = GT * P
PARTS = 3
LN_EPS = 1e-5
SCORE_SCALE = float(DK) ** 0.5


def build_program(nc, x, ctx_nat, ctx_t, mask_row, mask_col, mask_key, wq_t, wk_t, wv_t, wo_t,
                  router_t, router_bias, gate_w, up_w, down_w, ident, ident_bf, head_mask, half_mask, expert_sel,
                  expert_iota, out):
    stack = ExitStack()
    with stack:
        def sb(name, shape, dt=F32):
            return stack.enter_context(nc.sbuf_tensor(name, shape, dt))

        def sem(name):
            return stack.enter_context(nc.semaphore(name))

        ident_sb = sb("ident_sb", [P, P])
        identb_sb = sb("identb_sb", [P, P], BF16)
        hmask_sb = sb("hmask_sb", [P, HG])
        half_mask_sb = sb("half_mask_sb", [P, 2])
        iota_sb = sb("iota_sb", [P, EXPERTS])
        bias_sb = sb("bias_sb", [P, EXPERTS])
        sel_sb = sb("sel_sb", [PARTS * EXPERTS, EPAIRS, P], BF16)
        wq_sb = sb("wq_sb", [P, D])
        wk_sb = sb("wk_sb", [P, D])
        wv_sb = sb("wv_sb", [P, D])
        wo_sb = sb("wo_sb", [P, D])
        wr_sb = sb("wr_sb", [P, EXPERTS])
        gate_sb = sb("gate_sb", [P, UNITS, P])
        up_sb = sb("up_sb", [P, UNITS, P])
        down_sb = sb("down_sb", [P, UNITS, D])
        x_sb = sb("x_sb", [P, TILES, D])
        q_all = sb("q_all", [P, TILES, 2, S])
        k_all = sb("k_all", [P, TILES, 2, S])
        v_all = sb("v_all", [P, TILES, BPT, PAIRS, DV])
        mix_all = sb("mix_all", [P, TILES, P])
        xt2_all = sb("xt2_all", [P, TOKENS])
        logit_all = sb("logit_all", [P, TILES, EXPERTS])
        comb_t = sb("comb_t", [PARTS * EXPERTS, TOKENS], BF16)
        mrow8 = sb("mrow8", [P, TOKENS], U8)
        mcol8 = sb("mcol8", [P, TILES], U8)
        mkey8 = sb("mkey8", [P, BATCHES], U8)
        valid_col = sb("valid_col", [P, TILES])
        share_key = sb("share_key", [P, BATCHES])
        share_half = sb("share_half", [P, BATCHES, 2])
        n_masked = sb("n_masked", [P, BATCHES])
        n_valid = sb("n_valid", [P, BATCHES])
        inv_valid = sb("inv_valid", [P, BATCHES])
        none_valid = sb("none_valid", [P, BATCHES])
        xn = [sb(f"xn{p}", [P, GT, D]) for p in range(2)]
        ctx_sb = [sb(f"ctx_sb{p}", [P, GT, D]) for p in range(2)]
        ctxt_sb = [sb(f"ctxt_sb{p}", [P, GN]) for p in range(2)]
        xt_sb = [sb(f"xt_sb{p}", [P, GN]) for p in range(2)]
        cmix_sb = [sb(f"cmix_sb{p}", [P, GN]) for p in range(2)]
        stats1 = [sb(f"stats1_{p}", [P, GT, 6]) for p in range(2)]
        mv1 = [sb(f"mv1_{p}", [P, GT, 2]) for p in range(2)]
        rstd1 = [sb(f"rstd1_{p}", [P, GT]) for p in range(2)]
        veps1 = [sb(f"veps1_{p}", [P, GT]) for p in range(2)]
        neg_half = sb("neg_half", [P, GT])
        eps_sb = sb("eps_sb", [P, GT])
        pause = sb("pause", [P, 1])
        q_blk = [sb(f"q_blk{p}", [P, 2, BPT, S]) for p in range(2)]
        k_blk = [sb(f"k_blk{p}", [P, 2, HG, S]) for p in range(2)]
        v_blk = [sb(f"v_blk{p}", [P, BPT, PAIRS, 2, DV]) for p in range(2)]
        smax = [sb(f"smax{p}", [P, HEADS]) for p in range(2)]
        prob = [sb(f"prob{p}", [P, HEADS * S]) for p in range(2)]
        prob_t = [sb(f"prob_t{p}", [P, PAIRS, P]) for p in range(2)]
        inv_den = [sb(f"inv_den{p}", [P, HEADS]) for p in range(2)]
        att = [sb(f"att{p}", [P, HEADS, DK]) for p in range(2)]
        att_t = [sb(f"att_t{p}", [P, P]) for p in range(2)]
        stats2 = [sb(f"stats2_{p}", [P, 6]) for p in range(2)]
        mv2 = [sb(f"mv2_{p}", [P, 2]) for p in range(2)]
        veps2 = [sb(f"veps2_{p}", [P, 1]) for p in range(2)]
        rstd2 = [sb(f"rstd2_{p}", [P, 1]) for p in range(2)]
        xn2 = [sb(f"xn2_{p}", [P, D]) for p in range(2)]
        xt2 = [sb(f"xt2_{p}", [P, P]) for p in range(2)]
        top_v = sb("top_v", [P, TILES, 8])
        top_i = sb("top_i", [P, TILES, 8], U32)
        top_f = sb("top_f", [P, TILES, 2])
        gap = sb("gap", [P, TILES])
        second = sb("second", [P, TILES])
        den2 = sb("den2", [P, TILES])
        w_top = sb("w_top", [P, TILES, 2])
        comb = sb("comb", [P, TILES, EXPERTS])
        comb_b = sb("comb_b", [P, TILES, EXPERTS])
        comb3 = sb("comb3", [P, TILES, PARTS, EXPERTS], BF16)
        sig = [sb(f"sig{p}", [P, GN]) for p in range(2)]
        hid_u = [sb(f"hid_u{p}", [P, GN]) for p in range(2)]
        hid = [sb(f"hid{p}", [P, GN]) for p in range(2)]
        moe_t = sb("moe_t", [P, GN])

        banks = [stack.enter_context(nc.psum_tensor(f"bank{i}", [P, GN], F32)) for i in range(8)]

        s_x = [sem(f"s_xload{g}") for g in range(GROUPS)]
        s_const = sem("s_const")
        s_mask = sem("s_mask")
        s_wproj = sem("s_wproj")
        s_wmoe = sem("s_wmoe")
        s_ctx = [sem(f"s_ctx{p}") for p in range(2)]
        s_ctxt = [sem(f"s_ctxt{p}") for p in range(2)]
        s_valid = sem("s_valid")
        s_nmask = sem("s_nmask")
        s_cnt = sem("s_cnt")
        s_mix = sem("s_mix")
        s_zero = sem("s_zero")
        s_half = sem("s_half")
        s_share = sem("s_share")
        s_vden = sem("s_vden")
        s_stat1 = sem("s_stat1")
        s_mv1 = sem("s_mv1")
        s_veps1 = sem("s_veps1")
        s_rstd1 = sem("s_rstd1")
        s_xn = sem("s_xn")
        s_xt = sem("s_xt")
        s_xt_sb = sem("s_xt_sb")
        s_cmix = sem("s_cmix")
        s_cmix_sb = sem("s_cmix_sb")
        s_v = sem("s_v")
        s_v_act = sem("s_v_act")
        s_v_dve = sem("s_v_dve")
        s_q = sem("s_q")
        s_q_sb = sem("s_q_sb")
        s_k = sem("s_k")
        s_k_sb = sem("s_k_sb")
        s_blk = sem("s_blk")
        s_vblk = sem("s_vblk")
        s_score = sem("s_score")
        s_max = sem("s_max")
        s_sub = sem("s_sub")
        s_exp = sem("s_exp")
        s_pt = [sem(f"s_pt{h}") for h in range(2)]
        s_pt_sb = [sem(f"s_pt_sb{h}") for h in range(2)]
        s_pv = sem("s_pv")
        s_iden = sem("s_iden")
        s_att = sem("s_att")
        s_at = sem("s_at")
        s_at_sb = sem("s_at_sb")
        s_wo = sem("s_wo")
        s_x1 = sem("s_x1")
        s_stat2 = sem("s_stat2")
        s_mv2 = sem("s_mv2")
        s_veps2 = sem("s_veps2")
        s_rstd2 = sem("s_rstd2")
        s_xn2 = sem("s_xn2")
        s_xt2 = sem("s_xt2")
        s_xt2_sb = sem("s_xt2_sb")
        s_xt2_all = sem("s_xt2_all")
        s_logit = sem("s_logit")
        s_logit_sb = sem("s_logit_sb")
        s_route = sem("s_route")
        s_second = sem("s_second")
        s_gap = sem("s_gap")
        s_comb3 = sem("s_comb3")
        s_ct = sem("s_ct")
        s_ct_sb = sem("s_ct_sb")
        s_gate = sem("s_gate")
        s_up = sem("s_up")
        s_cb = sem("s_cb")
        s_sig = sem("s_sig")
        s_hid_u = sem("s_hid_u")
        s_hid = sem("s_hid")
        s_down = sem("s_down")
        s_moe_sb = sem("s_moe_sb")
        s_yt = sem("s_yt")
        s_y = sem("s_y")
        s_out = [sem(f"s_out{p}") for p in range(2)]

        x_view = x.rearrange("(t p) d -> p t d", p=P)
        ctx_view = ctx_nat.rearrange("(t p) d -> p t d", p=P)
        out_view = out.rearrange("(t p) d -> p t d", p=P)

        xt_ps, cmix_ps, v_ps, q_ps, k_ps = banks[0], banks[1], banks[2], banks[3], banks[4]
        score_ps = banks[0:2]
        pt_ps = banks[2:4]
        pv_ps = banks[4]
        at_ps = banks[5]
        wo_ps = banks[6]
        tail_ps = banks[7]
        gate_ps = banks[0:2]
        up_ps = banks[2:4]
        cb_ps = banks[4:6]
        moe_ps = banks[6]
        yt_ps = banks[7]

        def bank_bf16(bank):
            return bank[:, :].bitcast(BF16)

        def paired_loop(eng, first, last, step):
            assert (last - first) % 2 == 0
            with eng.Fori(0, (last - first) // 2) as i:
                for parity in range(2):
                    step(i * 2 + (first + parity), (first + parity) % 2)

        LEAD, TRAIL = -1, 2

        def pipeline(eng, step):
            def peel(t):
                step(t, t % 2, lambda lag: 0 <= t - lag < TILES)
            start, end = TRAIL, TILES - 2
            for t in range(LEAD, start):
                peel(t)
            with eng.Fori(0, (end - start) // 2) as i:
                for parity in range(2):
                    step(i * 2 + (start + parity), (start + parity) % 2, lambda lag: True)
            for t in range(end, TILES + TRAIL):
                peel(t)

        block = stack.enter_context(nc.Block())

        @block.sync
        def _(sp):
            for g in range(GROUPS):
                sp.dma_start(x_sb[:, g * GT:(g + 1) * GT, :], x_view[:, g * GT:(g + 1) * GT, :]).then_inc(s_x[g], 16)
                if g == 0:
                    sp.dma_start(ident_sb[:, :], ident).then_inc(s_const, 16)
                    sp.dma_start(hmask_sb[:, :], head_mask).then_inc(s_const, 16)
                    sp.dma_start(half_mask_sb[:, :], half_mask).then_inc(s_const, 16)
                    for p in range(2):
                        sp.dma_start(ctx_sb[p][:, :, :], ctx_view[:, p * GT:(p + 1) * GT, :]).then_inc(s_ctx[p], 16)
                        sp.dma_start(ctxt_sb[p][:, :], ctx_t[:, p * GN:(p + 1) * GN]).then_inc(s_ctxt[p], 16)
            for p in range(2):
                g = p + 2
                sp.wait_ge(s_cmix, g - 1)
                sp.dma_start(ctx_sb[p][:, :, :], ctx_view[:, g * GT:(g + 1) * GT, :]).then_inc(s_ctx[p], 16)
                sp.wait_ge(s_v, g - 1)
                sp.dma_start(ctxt_sb[p][:, :], ctx_t[:, g * GN:(g + 1) * GN]).then_inc(s_ctxt[p], 16)
            def store(g, p):
                sp.wait_ge(s_y, g + 1)
                sp.dma_start(out_view[:, bass.ds(g * GT, GT), :], x_sb[:, bass.ds(g * GT, GT), :]).then_inc(s_out[p], 16)
            paired_loop(sp, 0, GROUPS, store)
            for p in range(2):
                sp.wait_ge(s_out[p], 16 * GROUPS // 2)

        @block.gpsimd
        def _(pool):
            nc.gpsimd.memset(neg_half[:, :], -0.5).then_inc(s_half, 1)
            nc.gpsimd.memset(eps_sb[:, :], LN_EPS).then_inc(s_half, 1)
            nc.gpsimd.memset(mix_all[:, :, :], 0.0).then_inc(s_zero, 1)
            nc.gpsimd.memset(v_all[:, :, :, :, DK].rearrange("p t b j -> p (t b j)"), 1.0).then_inc(s_zero, 1)
            pool.wait_ge(s_half, 2)
            pool.wait_ge(s_zero, 2)

            def rstd1_of(g, p):
                pool.wait_ge(s_mv1, g + 1)
                nc.gpsimd.tensor_tensor(veps1[p][:, :], mv1[p][:, :, 1], eps_sb[:, :], ALU.add).then_inc(s_veps1, 1)
                pool.wait_ge(s_veps1, g + 1)
                nc.gpsimd.tensor_tensor(rstd1[p][:, :], veps1[p][:, :], neg_half[:, :], ALU.pow).then_inc(s_rstd1, 1)
            paired_loop(pool, 0, GROUPS, rstd1_of)
            pool.wait_ge(s_const, 48)
            pool.wait_ge(s_share, 2)
            pool.wait_ge(s_q_sb, GROUPS)
            pool.wait_ge(s_k_sb, GROUPS)
            pool.wait_ge(s_v_act, GROUPS)
            pool.wait_ge(s_v_dve, GROUPS)

            def blocks_of(t, p, first):
                if not first:
                    pool.wait_ge(s_score, t - 1)
                nc.gpsimd.tensor_tensor(
                    q_blk[p][:, :, :, :],
                    q_all[:, bass.ds(t, 1), :, :].rearrange("p o g (c s) -> p (o g) c s", c=1).broadcast_to([P, 2, BPT, S]),
                    half_mask_sb[:, :].rearrange("p (o b e) -> p o b e", o=1, e=1).broadcast_to([P, 2, BPT, S]), ALU.mult)
                for g in range(2):
                    last = nc.gpsimd.tensor_tensor(
                        k_blk[p][:, g, :, :],
                        k_all[:, bass.ds(t, 1), g, :].broadcast_to([P, HG, S]),
                        hmask_sb[:, :].rearrange("p (h o) -> p h o", o=1).broadcast_to([P, HG, S]), ALU.mult)
                last.then_inc(s_blk, 1)
                if not first:
                    pool.wait_ge(s_pv, t - 1)
                for b in range(BPT):
                    last = nc.gpsimd.tensor_tensor(
                        v_blk[p][:, b, :, :, :],
                        v_all[:, bass.ds(t, 1), b, :, :].rearrange("p o j (e d) -> p (o j) e d", e=1)
                        .broadcast_to([P, PAIRS, 2, DV]),
                        share_half[:, bass.ds(t * BPT + b, 1), :].rearrange("p o (e d) -> p o e d", d=1)
                        .broadcast_to([P, PAIRS, 2, DV]), ALU.mult)
                last.then_inc(s_vblk, 1)

            def step(t, p, on):
                if on(-2):
                    blocks_of(t + 2, p, first=isinstance(t, int) and t < 0)
                if on(1):
                    q = 1 - p
                    pool.wait_ge(s_mv2, t)
                    nc.gpsimd.tensor_tensor(veps2[q][:, :], mv2[q][:, 1:2], eps_sb[:, 0:1], ALU.add).then_inc(s_veps2, 1)
                    pool.wait_ge(s_veps2, t)
                    nc.gpsimd.tensor_tensor(rstd2[q][:, :], veps2[q][:, :], neg_half[:, 0:1],
                                            ALU.pow).then_inc(s_rstd2, 1)
                if on(2):
                    pool.wait_ge(s_xt2_sb, t - 1)
                    nc.gpsimd.tensor_copy(xt2_all[:, bass.ds((t - 2) * P, P)], xt2[p][:, :]).then_inc(s_xt2_all, 1)

            blocks_of(0, 0, first=True)
            pipeline(pool, step)

        @block.scalar
        def _(act):
            act.dma_start(mcol8[:, :], mask_col).then_inc(s_mask, 16)
            act.dma_start(mkey8[:, :], mask_key).then_inc(s_mask, 16)
            act.dma_start(mrow8[:, :], mask_row.broadcast_to([P, TOKENS])).then_inc(s_mask, 16)
            for dst, src in ((wq_sb, wq_t), (wk_sb, wk_t), (wv_sb, wv_t), (wo_sb, wo_t), (wr_sb, router_t),
                             (bias_sb, router_bias.broadcast_to([P, EXPERTS])), (identb_sb, ident_bf)):
                act.dma_start(dst[:, :], src).then_inc(s_wproj, 16)
            for dst, src in ((gate_sb, gate_w), (up_sb, up_w), (down_sb, down_w), (sel_sb, expert_sel)):
                act.dma_start(dst[:, :, :], src).then_inc(s_wmoe, 16)
            act.dma_start(iota_sb[:, :], expert_iota).then_inc(s_wmoe, 16)

            def project(g, p):
                act.wait_ge(s_xt, g + 1)
                nc.scalar.copy(xt_sb[p][:, :], xt_ps[:, :]).then_inc(s_xt_sb, 1)
                act.wait_ge(s_v, g + 1)
                for b in range(BPT):
                    last = nc.scalar.copy(
                        v_all[0:S, bass.ds(g * GT, GT), b, :, 0:DK],
                        v_ps[b * S:(b + 1) * S, :].rearrange("p (t j e d) -> p t j e d", t=GT, e=2, d=DK)[:, :, :, 0, :])
                last.then_inc(s_v_act, 1)
                act.wait_ge(s_q, g + 1)
                nc.scalar.copy(q_all[:, bass.ds(g * GT, GT), :, :].rearrange("p t g s -> p g t s"),
                               q_ps[:, :].rearrange("p (g t s) -> p g t s", g=2, t=GT)).then_inc(s_q_sb, 1)
            paired_loop(act, 0, GROUPS, project)

            def step(t, p, on):
                q = 1 - p
                if on(1):
                    act.wait_ge(s_at, t)
                    nc.scalar.copy(att_t[q][:, :], at_ps[:, 0:P]).then_inc(s_at_sb, 1)
                if on(0):
                    for h in range(2):
                        act.wait_ge(s_pt[h], t + 1)
                        nc.scalar.copy(prob_t[p][:, h * GT:(h + 1) * GT, :],
                                       pt_ps[h][:, :].rearrange("p (j q) -> p j q", q=P)).then_inc(s_pt_sb[h], 1)
                if on(2):
                    act.wait_ge(s_xt2, t - 1)
                    nc.scalar.copy(xt2[p][:, :], tail_ps[:, 0:P]).then_inc(s_xt2_sb, 1)
                if on(-1):
                    act.wait_ge(s_sub, t + 2)
                    nc.scalar.activation(prob[q][:, :], prob[q][:, :], ACT.Exp, scale=SCORE_SCALE).then_inc(s_exp, 1)
            pipeline(act, step)

            act.wait_ge(s_gap, 1)
            nc.scalar.activation(second[:, :], gap[:, :], ACT.Exp).then_inc(s_second, 1)
            for g in range(GROUPS):
                act.wait_ge(s_ct, g + 1)
                nc.scalar.copy(comb_t[:, g * GN:(g + 1) * GN],
                               bank_bf16(banks[g])[0:PARTS * EXPERTS, 0:GN]).then_inc(s_ct_sb, 1)

            def experts(g, p):
                for u in range(UNITS):
                    n, r = g * UNITS + u, (p * UNITS + u) % 2
                    act.wait_ge(s_gate, n + 1)
                    if u >= 2:
                        act.wait_ge(s_hid_u, n - 1)
                    nc.scalar.activation(sig[r][:, :], gate_ps[r][:, :], ACT.Silu).then_inc(s_sig, 1)
                act.wait_ge(s_down, (g + 1) * UNITS)
                nc.scalar.copy(moe_t[:, :], moe_ps[:, :]).then_inc(s_moe_sb, 1)
            paired_loop(act, 0, GROUPS, experts)

        @block.vector
        def _(dve):
            dve.wait_ge(s_mask, 48)
            nc.vector.tensor_scalar(valid_col[:, :], mcol8[:, :], -1.0, 1.0, ALU.mult, ALU.add).then_inc(s_valid, 1)
            nc.vector.tensor_scalar(share_key[:, :], mkey8[:, :], -1.0, 1.0, ALU.mult, ALU.add).then_inc(s_valid, 1)
            nc.vector.tensor_reduce(n_masked[:, :], mrow8[:, :].rearrange("p (b s) -> p b s", s=S), AX_X,
                                    ALU.add).then_inc(s_nmask, 1)
            dve.wait_ge(s_nmask, 1)
            nc.vector.tensor_scalar(n_valid[:, :], n_masked[:, :], -1.0, float(S), ALU.mult, ALU.add).then_inc(s_nmask, 1)
            nc.vector.tensor_scalar(none_valid[:, :], n_masked[:, :], float(S), None, ALU.is_equal).then_inc(s_nmask, 1)
            dve.wait_ge(s_nmask, 3)
            dve.wait_ge(s_valid, 2)
            nc.vector.tensor_scalar(n_valid[:, :], n_valid[:, :], 1.0, None, ALU.max).then_inc(s_cnt, 1)
            nc.vector.tensor_tensor(share_key[:, :], share_key[:, :], none_valid[:, :], ALU.add).then_inc(s_share, 1)
            dve.wait_ge(s_cnt, 1)
            nc.vector.reciprocal(inv_valid[:, :], n_valid[:, :]).then_inc(s_cnt, 1)
            dve.wait_ge(s_cnt, 2)
            dve.wait_ge(s_const, 48)
            dve.wait_ge(s_share, 1)
            nc.vector.tensor_tensor(
                share_half[:, :, :], share_key[:, :].rearrange("p (b o) -> p b o", o=1).broadcast_to([P, BATCHES, 2]),
                half_mask_sb[:, :].rearrange("p (o e) -> p o e", o=1).broadcast_to([P, BATCHES, 2]),
                ALU.mult).then_inc(s_share, 1)
            dve.wait_ge(s_zero, 2)
            halves = []
            for b in range(BPT):
                rows = slice(b * S, (b + 1) * S)
                blk = mix_all[rows, :, b * S:(b + 1) * S]
                halves.append((rows, blk))
                nc.vector.tensor_tensor(
                    blk, mrow8[rows, :].rearrange("p (t b s) -> p t b s", b=BPT, s=S)[:, :, b, :],
                    inv_valid[rows, :].rearrange("p (t b o) -> p t b o", b=BPT, o=1)[:, :, b, :].broadcast_to([S, TILES, S]),
                    ALU.mult).then_inc(s_mix, 1)
            dve.wait_ge(s_mix, 2)
            for b, (rows, blk) in enumerate(halves):
                nc.vector.tensor_tensor(
                    blk, blk,
                    ident_sb[rows, b * S:(b + 1) * S].rearrange("p (o s) -> p o s", o=1).broadcast_to([S, TILES, S]),
                    ALU.add).then_inc(s_mix, 1)
            dve.wait_ge(s_mix, 4)
            for rows, blk in halves:
                nc.vector.tensor_tensor(
                    blk, blk, valid_col[rows, :].rearrange("p (t o) -> p t o", o=1).broadcast_to([S, TILES, S]),
                    ALU.mult).then_inc(s_mix, 1)

            def norm1(g, p):
                if isinstance(g, int):
                    dve.wait_ge(s_x[g], 16)
                for i in range(GT):
                    nc.vector.bn_stats(stats1[p][:, i, :],
                                       x_sb[:, bass.ds(g * GT + i, 1), :].rearrange("p o d -> p (o d)")).then_inc(s_stat1, 1)
                dve.wait_ge(s_stat1, (g + 1) * GT)
                nc.vector.memset(pause[:, :], 0.0)
                for i in range(GT):
                    last = nc.vector.bn_aggr(mv1[p][:, i, :], stats1[p][:, i, :])
                last.then_inc(s_mv1, 1)
                dve.wait_ge(s_mv1, g + 1)
                dve.wait_ge(s_rstd1, g + 1)
                for i in range(GT):
                    last = nc.vector.tensor_scalar(
                        xn[p][:, i, :], x_sb[:, bass.ds(g * GT + i, 1), :].rearrange("p o d -> p (o d)"),
                        mv1[p][:, i, 0:1], rstd1[p][:, i:i + 1], ALU.subtract, ALU.mult)
                last.then_inc(s_xn, 1)

            def project(g, p):
                norm1(g, p)
                dve.wait_ge(s_cmix, g + 1)
                nc.vector.tensor_copy(cmix_sb[p][:, :], cmix_ps[:, :]).then_inc(s_cmix_sb, 1)
                dve.wait_ge(s_v_act, g + 1)
                for b in range(BPT):
                    last = nc.vector.tensor_copy(
                        v_all[S:P, bass.ds(g * GT, GT), b, :, 0:DK],
                        v_ps[b * S:(b + 1) * S, :].rearrange("p (t j e d) -> p t j e d", t=GT, e=2, d=DK)[:, :, :, 1, :])
                last.then_inc(s_v_dve, 1)
                dve.wait_ge(s_k, g + 1)
                nc.vector.tensor_copy(k_all[:, bass.ds(g * GT, GT), :, :].rearrange("p t g s -> p g t s"),
                                      k_ps[:, :].rearrange("p (g t s) -> p g t s", g=2, t=GT)).then_inc(s_k_sb, 1)
            for g in range(1, GROUPS):
                dve.wait_ge(s_x[g], 16)
            dve.wait_ge(s_x[0], 16)
            paired_loop(dve, 0, GROUPS, project)

            dve.wait_ge(s_wproj, 16 * 7)

            def step(t, p, on):
                q = 1 - p
                if on(1):
                    dve.wait_ge(s_pv, t)
                    pv = pv_ps[:, 0:HEADS * DV].rearrange("p (h d) -> p h d", d=DV)
                    nc.vector.reciprocal(inv_den[q][:, :], pv[:, :, DK]).then_inc(s_iden, 1)
                    dve.wait_ge(s_iden, t)
                    nc.vector.tensor_tensor(
                        att[q][:, :, :], pv[:, :, 0:DK],
                        inv_den[q][:, :].rearrange("p (h o) -> p h o", o=1).broadcast_to([P, HEADS, DK]),
                        ALU.mult).then_inc(s_att, 1)
                if on(-1):
                    dve.wait_ge(s_score, t + 2)
                    for g in range(2):
                        last = nc.vector.tensor_reduce(smax[q][:, g * HG:(g + 1) * HG],
                                                       score_ps[g][:, :].rearrange("p (h s) -> p h s", s=S), AX_X, ALU.max)
                    last.then_inc(s_max, 1)
                    dve.wait_ge(s_max, t + 2)
                    if not (isinstance(t, int) and t < 1):
                        dve.wait_ge(s_pt[1], t)
                    for g in range(2):
                        last = nc.vector.tensor_tensor(
                            prob[q][:, g * GN:(g + 1) * GN].rearrange("p (h s) -> p h s", s=S),
                            score_ps[g][:, :].rearrange("p (h s) -> p h s", s=S),
                            smax[q][:, g * HG:(g + 1) * HG].rearrange("p (h o) -> p h o", o=1).broadcast_to([P, HG, S]),
                            ALU.subtract)
                    last.then_inc(s_sub, 1)
                if on(1):
                    x1 = x_sb[:, bass.ds(t - 1, 1), :].rearrange("p o d -> p (o d)")
                    dve.wait_ge(s_wo, t)
                    nc.vector.tensor_tensor(x1, x1, wo_ps[:, 0:D], ALU.add).then_inc(s_x1, 1)
                    dve.wait_ge(s_x1, t)
                    nc.vector.memset(pause[:, :], 0.0)
                    nc.vector.bn_stats(stats2[q][:, :], x1).then_inc(s_stat2, 1)
                    dve.wait_ge(s_stat2, t)
                    nc.vector.memset(pause[:, :], 0.0)
                    nc.vector.bn_aggr(mv2[q][:, :], stats2[q][:, :]).then_inc(s_mv2, 1)
                    dve.wait_ge(s_mv2, t)
                    dve.wait_ge(s_rstd2, t)
                    nc.vector.tensor_scalar(xn2[q][:, :], x1, mv2[q][:, 0:1], rstd2[q][:, :], ALU.subtract,
                                            ALU.mult).then_inc(s_xn2, 1)
                if on(2):
                    dve.wait_ge(s_logit, t - 1)
                    nc.vector.tensor_tensor(logit_all[:, bass.ds(t - 2, 1), :].rearrange("p o e -> p (o e)"),
                                            tail_ps[:, 0:EXPERTS], bias_sb[:, :], ALU.add).then_inc(s_logit_sb, 1)
            pipeline(dve, step)

            done = [0]

            def chained(instruction):
                done[0] += 1
                instruction.then_inc(s_route, 1)
                dve.wait_ge(s_route, done[0])

            dve.wait_ge(s_logit_sb, TILES)
            dve.wait_ge(s_wmoe, 16 * 5)
            for t in range(TILES):
                last = nc.vector.max(top_v[:, t, :], logit_all[:, t, :])
            chained(last)
            for t in range(TILES):
                last = nc.vector.max_index(top_i[:, t, :], top_v[:, t, :], logit_all[:, t, :])
            nc.vector.tensor_tensor(gap[:, :], top_v[:, :, 1], top_v[:, :, 0], ALU.subtract).then_inc(s_gap, 1)
            chained(last)
            chained(nc.vector.tensor_copy(top_f[:, :, :], top_i[:, :, 0:2]))
            dve.wait_ge(s_second, 1)
            chained(nc.vector.tensor_scalar(den2[:, :], second[:, :], 1.0, None, ALU.add))
            chained(nc.vector.reciprocal(w_top[:, :, 0], den2[:, :]))
            chained(nc.vector.tensor_tensor(w_top[:, :, 1], second[:, :], w_top[:, :, 0], ALU.mult))
            iota_bc = iota_sb[:, :].rearrange("p (o e) -> p o e", o=1).broadcast_to([P, TILES, EXPERTS])
            for k, dst in ((0, comb), (1, comb_b)):
                chained(nc.vector.tensor_tensor(dst[:, :, :], iota_bc,
                                                top_f[:, :, k:k + 1].broadcast_to([P, TILES, EXPERTS]), ALU.is_equal))
                chained(nc.vector.tensor_tensor(dst[:, :, :], dst[:, :, :],
                                                w_top[:, :, k:k + 1].broadcast_to([P, TILES, EXPERTS]), ALU.mult))
            chained(nc.vector.tensor_tensor(comb[:, :, :], comb[:, :, :], comb_b[:, :, :], ALU.add))
            for part in range(PARTS):
                chained(nc.vector.tensor_copy(comb3[:, :, part, :], comb[:, :, :]))
                if part < PARTS - 1:
                    chained(nc.vector.tensor_tensor(comb[:, :, :], comb[:, :, :], comb3[:, :, part, :], ALU.subtract))
            nc.vector.tensor_copy(top_f[:, 0, 0:1], top_f[:, 0, 0:1]).then_inc(s_comb3, 1)

            def experts(g, p):
                for u in range(UNITS):
                    n, r = g * UNITS + u, (p * UNITS + u) % 2
                    routed = u < EPAIRS
                    dst = hid_u[r] if routed else hid[r]
                    dve.wait_ge(s_sig, n + 1)
                    dve.wait_ge(s_up, n + 1)
                    if u >= 2:
                        dve.wait_ge(s_down, n - 1)
                    nc.vector.tensor_tensor(dst[:, :], sig[r][:, :], up_ps[r][:, :], ALU.mult).then_inc(s_hid_u, 1)
                    if routed:
                        dve.wait_ge(s_hid_u, n + 1)
                        dve.wait_ge(s_cb, g * EPAIRS + u + 1)
                        nc.vector.tensor_tensor(hid[r][:, :], hid_u[r][:, :], cb_ps[r][:, :], ALU.mult).then_inc(s_hid, 1)
                dve.wait_ge(s_yt, g + 1)
                rows = x_sb[:, bass.ds(g * GT, GT), :]
                nc.vector.tensor_tensor(rows, yt_ps[:, :].rearrange("p (t d) -> p t d", d=D), rows,
                                        ALU.add).then_inc(s_y, 1)
            paired_loop(dve, 0, GROUPS, experts)

        @block.tensor
        def _(pe):
            pe.wait_ge(s_const, 48)
            pe.wait_ge(s_wproj, 16 * 7)
            pe.wait_ge(s_mix, 6)

            def project(g, p, first=False):
                k = 16 * (g // 2 + 1) if isinstance(g, int) else None
                pe.wait_ge(s_xn, g + 1)
                if not first:
                    pe.wait_ge(s_xt_sb, g)
                for i in range(GT):
                    last = nc.tensor.transpose(xt_ps[:, i * P:(i + 1) * P], xn[p][:, i, :], ident_sb[:, :])
                last.then_inc(s_xt, 1)
                pe.wait_ge(s_ctx[p], k)
                if not first:
                    pe.wait_ge(s_cmix_sb, g)
                for i in range(GT):
                    last = nc.tensor.matmul(cmix_ps[:, i * P:(i + 1) * P], ctx_sb[p][:, i, :], mix_all[:, g * GT + i, :],
                                            start=True, stop=True)
                last.then_inc(s_cmix, 1)
                pe.wait_ge(s_ctxt[p], k)
                if not first:
                    pe.wait_ge(s_v_act, g)
                    pe.wait_ge(s_v_dve, g)
                for i in range(GT):
                    last = nc.tensor.matmul(v_ps[:, i * P:(i + 1) * P], ctxt_sb[p][:, i * P:(i + 1) * P], wv_sb[:, :],
                                            start=True, stop=True)
                last.then_inc(s_v, 1)
                for w, src, have, dst, drained, made in ((wq_sb, xt_sb, s_xt_sb, q_ps, s_q_sb, s_q),
                                                        (wk_sb, cmix_sb, s_cmix_sb, k_ps, s_k_sb, s_k)):
                    pe.wait_ge(have, g + 1)
                    if not first:
                        pe.wait_ge(drained, g)
                    for hg in range(2):
                        for b in range(BPT):
                            last = nc.tensor.matmul(
                                dst[b * ROWS:(b + 1) * ROWS, hg * GT * S:(hg + 1) * GT * S],
                                w[:, hg * ROWS:(hg + 1) * ROWS],
                                src[p][:, :].rearrange("p (t b s) -> p t b s", b=BPT, s=S)[:, :, b, :],
                                start=True, stop=True)
                    last.then_inc(made, 1)
            for g in range(GROUPS):
                project(g, g % 2, first=g == 0)

            def step(t, p, on):
                q = 1 - p

                def transposes(h):
                    if not (isinstance(t, int) and t < 1):
                        pe.wait_ge(s_pt_sb[h], t)
                    for j in range(GT):
                        c = (h * GT + j) * P
                        last = nc.tensor.transpose(pt_ps[h][:, j * P:(j + 1) * P], prob[p][:, c:c + P], ident_sb[:, :])
                    last.then_inc(s_pt[h], 1)

                def values(b):
                    rows = slice(b * S, (b + 1) * S)
                    for j in range(PAIRS):
                        last = nc.tensor.matmul(
                            pv_ps[rows, j * 2 * DV:(j + 1) * 2 * DV], prob_t[p][:, j, b * S:(b + 1) * S],
                            v_blk[p][:, b, j, :, :].rearrange("p e d -> p (e d)"), start=True, stop=True)
                    return last

                if on(-1):
                    pe.wait_ge(s_blk, t + 2)
                    if not (isinstance(t, int) and t < 0):
                        pe.wait_ge(s_sub, t + 1)
                    for g in range(2):
                        last = nc.tensor.matmul(score_ps[g][:, :], q_blk[q][:, g, :, :].rearrange("p b s -> p (b s)"),
                                                k_blk[q][:, g, :, :].rearrange("p h s -> p (h s)"), start=True, stop=True)
                    last.then_inc(s_score, 1)
                if on(1):
                    pe.wait_ge(s_att, t)
                    if not (isinstance(t, int) and t < 2):
                        pe.wait_ge(s_at_sb, t - 1)
                    nc.tensor.transpose(at_ps[:, 0:P], att[q][:, :, :].rearrange("p h d -> p (h d)"),
                                        ident_sb[:, :]).then_inc(s_at, 1)
                if on(0):
                    pe.wait_ge(s_exp, t + 1)
                    transposes(0)
                if on(1):
                    pe.wait_ge(s_at_sb, t)
                    if not (isinstance(t, int) and t < 2):
                        pe.wait_ge(s_x1, t - 1)
                    nc.tensor.matmul(wo_ps[:, 0:D], att_t[q][:, :], wo_sb[:, :], start=True, stop=True).then_inc(s_wo, 1)
                if on(0):
                    transposes(1)
                if on(2):
                    pe.wait_ge(s_xn2, t - 1)
                    if not (isinstance(t, int) and t < 3):
                        pe.wait_ge(s_logit_sb, t - 2)
                    nc.tensor.transpose(tail_ps[:, 0:P], xn2[p][:, :], ident_sb[:, :]).then_inc(s_xt2, 1)
                if on(0):
                    pe.wait_ge(s_vblk, t + 1)
                    for h in range(2):
                        pe.wait_ge(s_pt_sb[h], t + 1)
                    if not (isinstance(t, int) and t < 1):
                        pe.wait_ge(s_att, t)
                    values(0)
                if on(2):
                    pe.wait_ge(s_xt2_sb, t - 1)
                    nc.tensor.matmul(tail_ps[:, 0:EXPERTS], xt2[p][:, :], wr_sb[:, :], start=True,
                                     stop=True).then_inc(s_logit, 1)
                if on(0):
                    values(1).then_inc(s_pv, 1)
            pipeline(pe, step)

            pe.wait_ge(s_comb3, 1)
            for g in range(GROUPS):
                for i in range(GT):
                    last = nc.tensor.transpose(bank_bf16(banks[g])[0:PARTS * EXPERTS, i * P:(i + 1) * P],
                                               comb3[:, g * GT + i, :, :].rearrange("p k e -> p (k e)"), identb_sb[:, :])
                last.then_inc(s_ct, 1)

            pe.wait_ge(s_xt2_all, TILES)
            pe.wait_ge(s_wmoe, 16 * 5)
            pe.wait_ge(s_ct_sb, GROUPS)

            def experts(g, p):
                cols = bass.ds(g * GN, GN)

                def down(u):
                    n, r = g * UNITS + u, (p * UNITS + u) % 2
                    if u < EPAIRS:
                        pe.wait_ge(s_hid, g * EPAIRS + u + 1)
                    else:
                        pe.wait_ge(s_hid_u, n + 1)
                    return nc.tensor.matmul(moe_ps[:, :], down_sb[:, u, :], hid[r][:, :], start=(u == 0),
                                            stop=(u == UNITS - 1)).then_inc(s_down, 1)

                for u in range(UNITS):
                    n, r = g * UNITS + u, (p * UNITS + u) % 2
                    if u >= 2:
                        pe.wait_ge(s_sig, n - 1)
                    nc.tensor.matmul(gate_ps[r][:, :], gate_sb[:, u, :], xt2_all[:, cols], start=True,
                                     stop=True).then_inc(s_gate, 1)
                    if u >= 2:
                        pe.wait_ge(s_hid_u, n - 1)
                        if u < EPAIRS:
                            pe.wait_ge(s_hid, g * EPAIRS + u - 1)
                    nc.tensor.matmul(up_ps[r][:, :], up_sb[:, u, :], xt2_all[:, cols], start=True,
                                     stop=True).then_inc(s_up, 1)
                    if u < EPAIRS:
                        nc.tensor.matmul(cb_ps[r][:, :], sel_sb[:, u, :], comb_t[:, cols], start=True,
                                         stop=True).then_inc(s_cb, 1)
                    if u:
                        down(u - 1)
                down(UNITS - 1)
                pe.wait_ge(s_moe_sb, g + 1)
                for i in range(GT):
                    last = nc.tensor.transpose(yt_ps[:, i * P:(i + 1) * P], moe_t[:, i * P:(i + 1) * P], ident_sb[:, :])
                last.then_inc(s_yt, 1)
            paired_loop(pe, 0, GROUPS, experts)


def host_layout(inputs):
    a = {k: np.asarray(v) for k, v in inputs.items()}
    c = np.ascontiguousarray
    mask = a["mask_Bx1x1xS2_bk0"].reshape(TOKENS)
    key_rows = mask.reshape(BATCHES, S).T
    ctx = a["ctx_1024"].reshape(TOKENS, D)

    def pairs(w):
        return w.transpose(1, 0, 2).reshape(D, EPAIRS, P)

    gate = np.concatenate([pairs(a["L0_ffn_gate_proj"]), a["L0_ffn_sh_gate"].T[:, None, :]], axis=1)
    up = np.concatenate([pairs(a["L0_ffn_up_proj"]), a["L0_ffn_sh_up"].T[:, None, :]], axis=1)
    down = np.concatenate([a["L0_ffn_down_proj"].reshape(EPAIRS, P, D).transpose(1, 0, 2),
                           a["L0_ffn_sh_down"].T[:, None, :]], axis=1)
    ident = np.eye(P, dtype=np.float32)
    head_of_row = (np.arange(P) % ROWS) // DK
    head_mask = (head_of_row[:, None] == np.arange(HG)[None, :]).astype(np.float32)
    expert_of_row = np.arange(PARTS * EXPERTS) % EXPERTS
    expert_of_col = (2 * np.arange(EPAIRS)[:, None] + np.arange(P)[None, :] // E_DIM)
    sel = expert_of_row[:, None, None] == expert_of_col[None]
    bf16 = mybir.dt.np(BF16)
    return {
        "x": c(a["x"].reshape(TOKENS, D)), "ctx_nat": c(ctx), "ctx_t": c(ctx.T),
        "mask_row": c(mask.reshape(1, TOKENS)), "mask_col": c(mask.reshape(TILES, P).T),
        "mask_key": c(np.concatenate([key_rows, key_rows], axis=0)),
        "wq_t": c(a["L0_xattn_Wq"].T), "wk_t": c(a["L0_xattn_Wk"].T), "wv_t": c(a["L0_xattn_Wv"].T),
        "wo_t": c(a["L0_xattn_Wo"].T), "router_t": c(a["L0_ffn_router_w"].T),
        "router_bias": c(a["L0_ffn_router_bias"].reshape(1, EXPERTS)),
        "gate_w": c(gate), "up_w": c(up), "down_w": c(down),
        "ident": ident, "ident_bf": ident.astype(bf16), "head_mask": head_mask,
        "half_mask": (np.arange(P)[:, None] // S == np.arange(2)[None, :]).astype(np.float32),
        "expert_sel": sel.astype(bf16),
        "expert_iota": np.tile(np.arange(EXPERTS, dtype=np.float32), (P, 1)),
    }


def kernel(**inputs):
    import concourse.bacc as bacc
    from concourse.bass_utils import run_bass_kernel_spmd

    nc = bacc.Bacc("TRN2", target_bir_lowering=False, num_devices=1)
    arrays = host_layout(inputs)
    args = {n: nc.dram_tensor(n, a.shape, mybir.dt.from_np(a.dtype), kind="ExternalInput").ap()
            for n, a in arrays.items()}
    out = nc.dram_tensor("out", (TOKENS, D), F32, kind="ExternalOutput").ap()
    build_program(nc, out=out, **args)
    r = run_bass_kernel_spmd(nc, [arrays], core_ids=[0])
    return r.results[0]["out"].reshape(BATCHES, S, D)
```

```python
from contextlib import ExitStack

import numpy as np

import concourse.bass as bass
from concourse import mybir

F32 = mybir.dt.float32
F32R = mybir.dt.float32r
BF16 = mybir.dt.bfloat16
U8 = mybir.dt.uint8
U32 = mybir.dt.uint32
ALU = mybir.AluOpType
ACT = mybir.ActivationFunctionType
AX_X = mybir.AxisListType.X

P = 128
BATCHES, S, D = 32, 64, 128
HEADS, DK = 16, 8
TOKENS = BATCHES * S
TILES = TOKENS // P
BPT = P // S
HG = HEADS // 2
ROWS = HG * DK
PAIRS = HEADS // 2
DV = DK + 1
EXPERTS, E_DIM = 16, 64
EPAIRS = EXPERTS // 2
UNITS = EPAIRS + 1
GT = 4
GROUPS = TILES // GT
GN = GT * P
PARTS = 3
LN_EPS = 1e-5
W_MOE = 3 * UNITS * P
W_STEP = W_MOE // TILES
SCORE_SCALE = float(DK) ** 0.5


def build_program(nc, x, ctx_nat, ctx_t, mask_row, mask_col, w_att, router_bias, w_moe, consts, ident_bf,
                  expert_sel, out):
    stack = ExitStack()
    with stack:
        def sb(name, shape, dt=F32):
            return stack.enter_context(nc.sbuf_tensor(name, shape, dt))

        def sem(name):
            return stack.enter_context(nc.semaphore(name))

        consts_sb = sb("consts_sb", [P, P + HG + 2 + EXPERTS])
        ident_sb = consts_sb[:, 0:P]
        hmask_sb = consts_sb[:, P:P + HG]
        half_mask_sb = consts_sb[:, P + HG:P + HG + 2]
        iota_sb = consts_sb[:, P + HG + 2:]
        identb_sb = sb("identb_sb", [P, P], BF16)
        bias_sb = sb("bias_sb", [P, EXPERTS])
        sel_sb = sb("sel_sb", [PARTS * EXPERTS, EPAIRS, P], BF16)
        w_att_sb = sb("w_att_sb", [P, 4 * D + EXPERTS])
        wq_sb, wk_sb, wv_sb, wo_sb = (w_att_sb[:, i * D:(i + 1) * D] for i in range(4))
        wr_sb = w_att_sb[:, 4 * D:]
        w_moe_sb = sb("w_moe_sb", [P, W_MOE])
        w_hi = sb("w_hi", [P, W_MOE], F32R)
        w_lo = sb("w_lo", [P, W_MOE], F32R)
        x_sb = sb("x_sb", [P, TILES, D])
        q_all = sb("q_all", [P, TILES, 2, S])
        k_all = sb("k_all", [P, TILES, 2, S])
        v_all = sb("v_all", [P, TILES, BPT, PAIRS, DV])
        mix_all = sb("mix_all", [P, TILES, P])
        xt2_hi = sb("xt2_hi", [P, TOKENS], F32R)
        xt2_lo = sb("xt2_lo", [P, TOKENS], F32R)
        comb_t = sb("comb_t", [PARTS * EXPERTS, TOKENS], BF16)
        mrow8 = sb("mrow8", [P, TOKENS], U8)
        mcol8 = sb("mcol8", [P, TILES + BATCHES], U8)
        valid_col = sb("valid_col", [P, TILES])
        share_key = sb("share_key", [P, BATCHES])
        share_half = sb("share_half", [P, BATCHES, 2])
        n_masked = sb("n_masked", [P, BATCHES])
        n_valid = sb("n_valid", [P, BATCHES])
        inv_valid = sb("inv_valid", [P, BATCHES])
        inv_half = sb("inv_half", [P, BATCHES])
        none_valid = sb("none_valid", [P, BATCHES])
        xn = [sb(f"xn{p}", [P, GT, D]) for p in range(2)]
        ctx_sb = [sb(f"ctx_sb{p}", [P, GT, D]) for p in range(2)]
        ctxv_sb = [sb(f"ctxv_sb{p}", [P, GT, D]) for p in range(2)]
        ctxt_sb = [sb(f"ctxt_sb{p}", [P, GN]) for p in range(2)]
        xt_sb = [sb(f"xt_sb{p}", [P, GN]) for p in range(2)]
        cmix_sb = [sb(f"cmix_sb{p}", [P, GN]) for p in range(2)]
        stats1 = [sb(f"stats1_{p}", [P, GT, 6]) for p in range(2)]
        mv1 = [sb(f"mv1_{p}", [P, GT, 2]) for p in range(2)]
        rstd1 = [sb(f"rstd1_{p}", [P, GT]) for p in range(2)]
        veps1 = [sb(f"veps1_{p}", [P, GT]) for p in range(2)]
        neg_half = sb("neg_half", [P, GT])
        eps_sb = sb("eps_sb", [P, GT])
        pause = sb("pause", [P, 8])
        q_blk = [sb(f"q_blk{p}", [P, 2, BPT, S]) for p in range(2)]
        k_blk = [sb(f"k_blk{p}", [P, 2, HG, S]) for p in range(2)]
        v_blk = [sb(f"v_blk{p}", [P, BPT, PAIRS, 2, DV]) for p in range(2)]
        smax = [sb(f"smax{p}", [P, HEADS]) for p in range(2)]
        prob = [sb(f"prob{p}", [P, HEADS * S]) for p in range(2)]
        prob_t = [sb(f"prob_t{p}", [P, PAIRS, P]) for p in range(2)]
        inv_den = [sb(f"inv_den{p}", [P, HEADS]) for p in range(2)]
        att = [sb(f"att{p}", [P, HEADS, DK]) for p in range(2)]
        att_t = [sb(f"att_t{p}", [P, P]) for p in range(2)]
        stats2 = [sb(f"stats2_{p}", [P, 6]) for p in range(2)]
        mv2 = [sb(f"mv2_{p}", [P, 2]) for p in range(2)]
        veps2 = [sb(f"veps2_{p}", [P, 1]) for p in range(2)]
        rstd2 = [sb(f"rstd2_{p}", [P, 1]) for p in range(2)]
        xn2 = [sb(f"xn2_{p}", [P, D]) for p in range(2)]
        xt2 = [sb(f"xt2_{p}", [P, P]) for p in range(2)]
        logit = [sb(f"logit{p}", [P, EXPERTS]) for p in range(2)]
        top_v = [sb(f"top_v{p}", [P, 8]) for p in range(2)]
        top_i = [sb(f"top_i{p}", [P, 8], U32) for p in range(2)]
        top_f = sb("top_f", [P, TILES, 2])
        gap = sb("gap", [P, TILES])
        second = sb("second", [P, TILES])
        den2 = sb("den2", [P, TILES])
        w_top = sb("w_top", [P, TILES, 2])
        comb = sb("comb", [P, TILES, EXPERTS])
        comb_b = sb("comb_b", [P, TILES, EXPERTS])
        comb3 = sb("comb3", [P, TILES, PARTS, EXPERTS], BF16)
        sig = [sb(f"sig{p}", [P, GN]) for p in range(2)]
        hid_u = [sb(f"hid_u{p}", [P, GN]) for p in range(2)]
        hid = [sb(f"hid{p}", [P, GN]) for p in range(2)]
        hid_hi = [sb(f"hid_hi{p}", [P, GN], F32R) for p in range(2)]
        hid_lo = [sb(f"hid_lo{p}", [P, GN], F32R) for p in range(2)]
        moe_t = [sb(f"moe_t{p}", [P, GN]) for p in range(2)]

        banks = [stack.enter_context(nc.psum_tensor(f"bank{i}", [P, GN], F32)) for i in range(8)]

        s_x = [sem(f"s_xload{g}") for g in range(GROUPS)]
        s_const = sem("s_const")
        s_mask = sem("s_mask")
        s_wproj = sem("s_wproj")
        s_wmoe = sem("s_wmoe")
        s_ctx = [sem(f"s_ctx{p}") for p in range(2)]
        s_ctxt = [sem(f"s_ctxt{p}") for p in range(2)]
        s_valid = sem("s_valid")
        s_nmask = sem("s_nmask")
        s_cnt = sem("s_cnt")
        s_ihalf = sem("s_ihalf")
        s_vcol = sem("s_vcol")
        s_ctxv = sem("s_ctxv")
        s_mrow = sem("s_mrow")
        s_mean = sem("s_mean")
        s_mix = sem("s_mix")
        s_zero = sem("s_zero")
        s_half = sem("s_half")
        s_share = sem("s_share")
        s_vden = sem("s_vden")
        s_stat1 = sem("s_stat1")
        s_mv1 = sem("s_mv1")
        s_veps1 = sem("s_veps1")
        s_rstd1 = sem("s_rstd1")
        s_xn = sem("s_xn")
        s_xt = sem("s_xt")
        s_xt_sb = sem("s_xt_sb")
        s_cmix = sem("s_cmix")
        s_cmix_sb = sem("s_cmix_sb")
        s_v = sem("s_v")
        s_v_act = sem("s_v_act")
        s_v_dve = sem("s_v_dve")
        s_q = sem("s_q")
        s_q_sb = sem("s_q_sb")
        s_k = sem("s_k")
        s_k_sb = sem("s_k_sb")
        s_blk = sem("s_blk")
        s_vblk = sem("s_vblk")
        s_score = sem("s_score")
        s_max = sem("s_max")
        s_sub = sem("s_sub")
        s_exp = sem("s_exp")
        s_pt = [sem(f"s_pt{h}") for h in range(2)]
        s_pt_sb = [sem(f"s_pt_sb{h}") for h in range(2)]
        s_pv = sem("s_pv")
        s_iden = sem("s_iden")
        s_att = sem("s_att")
        s_at = sem("s_at")
        s_at_sb = sem("s_at_sb")
        s_wo = sem("s_wo")
        s_x1 = sem("s_x1")
        s_stat2 = sem("s_stat2")
        s_mv2 = sem("s_mv2")
        s_veps2 = sem("s_veps2")
        s_rstd2 = sem("s_rstd2")
        s_xn2 = sem("s_xn2")
        s_xt2 = sem("s_xt2")
        s_xt2_sb = sem("s_xt2_sb")
        s_xt2_hi = sem("s_xt2_hi")
        s_xt2_lo = sem("s_xt2_lo")
        s_w_hi = sem("s_w_hi")
        s_w_lo = sem("s_w_lo")
        s_logit = sem("s_logit")
        s_logit_sb = sem("s_logit_sb")
        s_top_v = sem("s_top_v")
        s_top_i = sem("s_top_i")
        s_top_f = sem("s_top_f")
        s_route = sem("s_route")
        s_second = sem("s_second")
        s_comb3 = sem("s_comb3")
        s_ct = sem("s_ct")
        s_ct_sb = sem("s_ct_sb")
        s_gate = sem("s_gate")
        s_up = sem("s_up")
        s_cb = sem("s_cb")
        s_sig = sem("s_sig")
        s_hid_u = sem("s_hid_u")
        s_hid = sem("s_hid")
        s_hid_hi = sem("s_hid_hi")
        s_hid_lo = sem("s_hid_lo")
        s_down = sem("s_down")
        s_moe_sb = sem("s_moe_sb")
        s_yt = sem("s_yt")
        s_y = sem("s_y")
        s_out = [sem(f"s_out{p}") for p in range(2)]

        x_view = x.rearrange("(t p) d -> p t d", p=P)
        ctx_view = ctx_nat.rearrange("(t p) d -> p t d", p=P)
        out_view = out.rearrange("(t p) d -> p t d", p=P)

        xt_ps, cmix_ps, v_ps, q_ps, k_ps = banks[0], banks[1], banks[2], banks[3], banks[4]
        score_ps = banks[0:2]
        pt_ps = banks[2:4]
        pv_ps = banks[4]
        at_ps = banks[5]
        wo_ps = banks[6]
        tail_ps = banks[7]
        gate_ps = banks[0:2]
        up_ps = banks[2:4]
        cb_ps = banks[4:6]
        moe_ps = banks[6]
        yt_ps = banks[7]

        def bank_bf16(bank):
            return bank[:, :].bitcast(BF16)

        def paired_loop(eng, first, last, step):
            assert (last - first) % 2 == 0
            with eng.Fori(0, (last - first) // 2) as i:
                for parity in range(2):
                    step(i * 2 + (first + parity), (first + parity) % 2)

        LEAD, TRAIL = -1, 2

        def pipeline(eng, step):
            def peel(t):
                step(t, t % 2, lambda lag: 0 <= t - lag < TILES)
            start, end = TRAIL, TILES - 2
            for t in range(LEAD, start):
                peel(t)
            with eng.Fori(0, (end - start) // 2) as i:
                for parity in range(2):
                    step(i * 2 + (start + parity), (start + parity) % 2, lambda lag: True)
            for t in range(end, TILES + TRAIL):
                peel(t)

        BODY = 2 * UNITS

        def expert_bodies(eng, body):
            with eng.Fori(0, GROUPS // 2) as i:
                body(i)

        def group_of(i, m):
            return i * 2 + m // UNITS, m % UNITS

        def wait_hid(eng, i, m):
            g, u = group_of(i, m)
            if u < EPAIRS:
                eng.wait_ge(s_hid, g * EPAIRS + u + 1)
            else:
                eng.wait_ge(s_hid_u, i * BODY + m + 1)

        def w_slice(w, u, kind):
            c = (3 * u + kind) * P
            return w[:, c:c + P]

        block = stack.enter_context(nc.Block())

        @block.sync
        def _(sp):
            sp.dma_start(x_sb[:, 0:GT, :], x_view[:, 0:GT, :]).then_inc(s_x[0], 16)
            sp.dma_start(consts_sb[:, :], consts).then_inc(s_const, 16)
            for p in range(2):
                sp.dma_start(ctx_sb[p][:, :, :], ctx_view[:, p * GT:(p + 1) * GT, :]).then_inc(s_ctx[p], 16)
                sp.dma_start(ctxt_sb[p][:, :], ctx_t[:, p * GN:(p + 1) * GN]).then_inc(s_ctxt[p], 16)
                sp.dma_start(x_sb[:, (p + 1) * GT:(p + 2) * GT, :], x_view[:, (p + 1) * GT:(p + 2) * GT, :]).then_inc(s_x[p + 1], 16)
            sp.dma_start(x_sb[:, 3 * GT:, :], x_view[:, 3 * GT:, :]).then_inc(s_x[3], 16)
            for p in range(2):
                g = p + 2
                sp.wait_ge(s_ctxv, g - 1)
                sp.dma_start(ctx_sb[p][:, :, :], ctx_view[:, g * GT:(g + 1) * GT, :]).then_inc(s_ctx[p], 16)
                sp.wait_ge(s_v, g - 1)
                sp.dma_start(ctxt_sb[p][:, :], ctx_t[:, g * GN:(g + 1) * GN]).then_inc(s_ctxt[p], 16)
            sp.dma_start(w_moe_sb[:, :], w_moe).then_inc(s_wmoe, 16)
            sp.dma_start(sel_sb[:, :, :], expert_sel).then_inc(s_wmoe, 16)
            sp.dma_start(identb_sb[:, :], ident_bf).then_inc(s_wmoe, 16)
            def store(g, p):
                sp.wait_ge(s_y, g + 1)
                sp.dma_start(out_view[:, bass.ds(g * GT, GT), :], x_sb[:, bass.ds(g * GT, GT), :]).then_inc(s_out[p], 16)
            paired_loop(sp, 0, GROUPS, store)
            for p in range(2):
                sp.wait_ge(s_out[p], 16 * GROUPS // 2)

        @block.gpsimd
        def _(pool):
            nc.gpsimd.memset(neg_half[:, :], -0.5).then_inc(s_half, 1)
            nc.gpsimd.memset(eps_sb[:, :], LN_EPS).then_inc(s_half, 1)
            nc.gpsimd.memset(v_all[:, :, :, :, DK].rearrange("p t b j -> p (t b j)"), 1.0).then_inc(s_zero, 1)
            pool.wait_ge(s_half, 2)
            pool.wait_ge(s_zero, 1)

            def rstd1_of(g):
                p = g % 2
                pool.wait_ge(s_mv1, g + 1)
                nc.gpsimd.tensor_tensor(veps1[p][:, :], mv1[p][:, :, 1], eps_sb[:, :], ALU.add).then_inc(s_veps1, 1)
                pool.wait_ge(s_veps1, g + 1)
                nc.gpsimd.tensor_tensor(rstd1[p][:, :], veps1[p][:, :], neg_half[:, :], ALU.pow).then_inc(s_rstd1, 1)

            rstd1_of(0)
            pool.wait_ge(s_mask, 32)
            pool.wait_ge(s_const, 16)
            pool.wait_ge(s_ihalf, 1)
            for g in range(GROUPS):
                mix = mix_all[:, g * GT:(g + 1) * GT, :]
                blk = mix.rearrange("p t (b s) -> p (t b) s", b=BPT)
                pool.wait_ge(s_mrow, g + 1)
                nc.gpsimd.tensor_tensor(
                    blk, blk,
                    inv_half[:, g * GT * BPT:(g + 1) * GT * BPT].rearrange("p (b o) -> p b o", o=1)
                    .broadcast_to([P, GT * BPT, S]), ALU.mult).then_inc(s_mean, 1)
                pool.wait_ge(s_mean, g + 1)
                nc.gpsimd.tensor_tensor(mix, mix, ident_sb.rearrange("p (o s) -> p o s", o=1).broadcast_to([P, GT, P]),
                                        ALU.add).then_inc(s_mix, 1)
                if g + 1 < GROUPS:
                    rstd1_of(g + 1)
            pool.wait_ge(s_const, 16)
            pool.wait_ge(s_share, 2)
            pool.wait_ge(s_q_sb, GROUPS)
            pool.wait_ge(s_k_sb, GROUPS)
            pool.wait_ge(s_v_act, GROUPS)
            pool.wait_ge(s_v_dve, GROUPS)

            def blocks_of(t, p, first):
                if not first:
                    pool.wait_ge(s_score, t - 1)
                nc.gpsimd.tensor_tensor(
                    q_blk[p][:, :, :, :],
                    q_all[:, bass.ds(t, 1), :, :].rearrange("p o g (c s) -> p (o g) c s", c=1).broadcast_to([P, 2, BPT, S]),
                    half_mask_sb.rearrange("p (o b e) -> p o b e", o=1, e=1).broadcast_to([P, 2, BPT, S]), ALU.mult)
                for g in range(2):
                    last = nc.gpsimd.tensor_tensor(
                        k_blk[p][:, g, :, :],
                        k_all[:, bass.ds(t, 1), g, :].broadcast_to([P, HG, S]),
                        hmask_sb.rearrange("p (h o) -> p h o", o=1).broadcast_to([P, HG, S]), ALU.mult)
                last.then_inc(s_blk, 1)
                if not first:
                    pool.wait_ge(s_pv, t - 1)
                for b in range(BPT):
                    last = nc.gpsimd.tensor_tensor(
                        v_blk[p][:, b, :, :, :],
                        v_all[:, bass.ds(t, 1), b, :, :].rearrange("p o j (e d) -> p (o j) e d", e=1)
                        .broadcast_to([P, PAIRS, 2, DV]),
                        share_half[:, bass.ds(t * BPT + b, 1), :].rearrange("p o (e d) -> p o e d", d=1)
                        .broadcast_to([P, PAIRS, 2, DV]), ALU.mult)
                last.then_inc(s_vblk, 1)

            def step(t, p, on):
                if on(-2):
                    blocks_of(t + 2, p, first=isinstance(t, int) and t < 0)
                if on(1):
                    q = 1 - p
                    pool.wait_ge(s_mv2, t)
                    nc.gpsimd.tensor_tensor(veps2[q][:, :], mv2[q][:, 1:2], eps_sb[:, 0:1], ALU.add).then_inc(s_veps2, 1)
                    pool.wait_ge(s_veps2, t)
                    nc.gpsimd.tensor_tensor(rstd2[q][:, :], veps2[q][:, :], neg_half[:, 0:1],
                                            ALU.pow).then_inc(s_rstd2, 1)
                if on(2):
                    cols = bass.ds((t - 2) * P, P)
                    pool.wait_ge(s_xt2_hi, t - 1)
                    nc.gpsimd.tensor_tensor(xt2_lo[:, cols], xt2[p][:, :], xt2_hi[:, cols].bitcast(F32),
                                            ALU.subtract).then_inc(s_xt2_lo, 1)

            blocks_of(0, 0, first=True)
            pipeline(pool, step)

        @block.scalar
        def _(act):
            act.dma_start(mcol8[:, :], mask_col).then_inc(s_mask, 16)
            act.dma_start(mrow8[:, :], mask_row.broadcast_to([P, TOKENS])).then_inc(s_mask, 16)
            act.dma_start(w_att_sb[:, :], w_att).then_inc(s_wproj, 16)
            act.dma_start(bias_sb[:, :], router_bias.broadcast_to([P, EXPERTS])).then_inc(s_wproj, 16)

            def mask_row_of(g):
                nc.scalar.copy(mix_all[:, g * GT:(g + 1) * GT, :].rearrange("p t k -> p (t k)"),
                               mrow8[:, g * GN:(g + 1) * GN]).then_inc(s_mrow, 1)

            act.wait_ge(s_mask, 32)
            mask_row_of(0)
            act.wait_ge(s_vcol, 1)

            def mask_ctx(g):
                act.wait_ge(s_ctx[g % 2], 16 * (g // 2 + 1))
                if g >= 2:
                    act.wait_ge(s_cmix, g - 1)
                for i in range(GT):
                    last = nc.scalar.mul(ctxv_sb[g % 2][:, i, :], ctx_sb[g % 2][:, i, :],
                                         valid_col[:, g * GT + i:g * GT + i + 1])
                last.then_inc(s_ctxv, 1)

            def project(g, p):
                act.wait_ge(s_xt, g + 1)
                nc.scalar.copy(xt_sb[p][:, :], xt_ps[:, :]).then_inc(s_xt_sb, 1)
                act.wait_ge(s_v, g + 1)
                for b in range(BPT):
                    last = nc.scalar.copy(
                        v_all[0:S, bass.ds(g * GT, GT), b, :, 0:DK],
                        v_ps[b * S:(b + 1) * S, :].rearrange("p (t j e d) -> p t j e d", t=GT, e=2, d=DK)[:, :, :, 0, :])
                last.then_inc(s_v_act, 1)
                act.wait_ge(s_q, g + 1)
                nc.scalar.copy(q_all[:, bass.ds(g * GT, GT), :, :].rearrange("p t g s -> p g t s"),
                               q_ps[:, :].rearrange("p (g t s) -> p g t s", g=2, t=GT)).then_inc(s_q_sb, 1)
            mask_ctx(0)
            for g in range(1, GROUPS):
                mask_row_of(g)
            for g in range(GROUPS):
                if g + 1 < GROUPS:
                    mask_ctx(g + 1)
                project(g, g % 2)

            def step(t, p, on):
                q = 1 - p
                if on(1):
                    act.wait_ge(s_at, t)
                    nc.scalar.copy(att_t[q][:, :], at_ps[:, 0:P]).then_inc(s_at_sb, 1)
                if on(0):
                    for h in range(2):
                        act.wait_ge(s_pt[h], t + 1)
                        nc.scalar.copy(prob_t[p][:, h * GT:(h + 1) * GT, :],
                                       pt_ps[h][:, :].rearrange("p (j q) -> p j q", q=P)).then_inc(s_pt_sb[h], 1)
                if on(2):
                    act.wait_ge(s_xt2, t - 1)
                    cols = bass.ds((t - 2) * P, P)
                    nc.scalar.copy(xt2[p][:, :], tail_ps[:, 0:P]).then_inc(s_xt2_sb, 1)
                    nc.scalar.copy(xt2_hi[:, cols], tail_ps[:, 0:P]).then_inc(s_xt2_hi, 1)
                if on(0):
                    cols = bass.ds(t * W_STEP, W_STEP)
                    nc.scalar.copy(w_hi[:, cols], w_moe_sb[:, cols]).then_inc(s_w_hi, 1)
                if on(-1):
                    act.wait_ge(s_sub, t + 2)
                    nc.scalar.activation(prob[q][:, :], prob[q][:, :], ACT.Exp, scale=SCORE_SCALE).then_inc(s_exp, 1)
            act.wait_ge(s_wmoe, 48)
            pipeline(act, step)

            act.wait_ge(s_top_f, TILES)
            nc.scalar.activation(second[:, :], gap[:, :], ACT.Exp).then_inc(s_second, 1)
            for g in range(GROUPS):
                act.wait_ge(s_ct, g + 1)
                nc.scalar.copy(comb_t[:, g * GN:(g + 1) * GN],
                               bank_bf16(banks[g])[0:PARTS * EXPERTS, 0:GN]).then_inc(s_ct_sb, 1)

            def body(i):
                for m in range(BODY + 1):
                    n, r = i * BODY + m, m % 2
                    if m in (UNITS + 2, ):
                        act.wait_ge(s_down, n - 2)
                        nc.scalar.copy(moe_t[0][:, :], moe_ps[:, :]).then_inc(s_moe_sb, 1)
                    if m < BODY:
                        act.wait_ge(s_gate, n + 1)
                        if m >= 2:
                            act.wait_ge(s_hid_u, n - 1)
                        nc.scalar.activation(sig[r][:, :], gate_ps[r][:, :], ACT.Silu).then_inc(s_sig, 1)
                    if m >= 1:
                        q = 1 - r
                        wait_hid(act, i, m - 1)
                        if m >= 3:
                            act.wait_ge(s_down, n - 2)
                        nc.scalar.copy(hid_hi[q][:, :], hid[q][:, :]).then_inc(s_hid_hi, 1)
                act.wait_ge(s_down, i * BODY + BODY)
                nc.scalar.copy(moe_t[1][:, :], moe_ps[:, :]).then_inc(s_moe_sb, 1)
            expert_bodies(act, body)

        @block.vector
        def _(dve):
            def norm1(g, p):
                dve.wait_ge(s_x[g], 16)
                for i in range(GT):
                    nc.vector.bn_stats(stats1[p][:, i, :], x_sb[:, g * GT + i, :]).then_inc(s_stat1, 1)
                dve.wait_ge(s_stat1, (g + 1) * GT)
                for i in range(GT):
                    last = nc.vector.bn_aggr(mv1[p][:, i, :], stats1[p][:, i, :])
                last.then_inc(s_mv1, 1)

            def scale1(g, p):
                dve.wait_ge(s_mv1, g + 1)
                dve.wait_ge(s_rstd1, g + 1)
                if g >= 2:
                    dve.wait_ge(s_xt, g - 1)
                for i in range(GT):
                    last = nc.vector.tensor_scalar(xn[p][:, i, :], x_sb[:, g * GT + i, :], mv1[p][:, i, 0:1],
                                                   rstd1[p][:, i:i + 1], ALU.subtract, ALU.mult)
                last.then_inc(s_xn, 1)

            norm1(0, 0)
            dve.wait_ge(s_mask, 32)
            nc.vector.tensor_scalar(valid_col[:, :], mcol8[:, 0:TILES], -1.0, 1.0, ALU.mult, ALU.add).then_inc(s_vcol, 1)
            nc.vector.tensor_scalar(share_key[:, :], mcol8[:, TILES:], -1.0, 1.0, ALU.mult, ALU.add).then_inc(s_valid, 1)
            nc.vector.tensor_reduce(n_masked[:, :], mrow8[:, :].rearrange("p (b s) -> p b s", s=S), AX_X,
                                    ALU.add).then_inc(s_nmask, 1)
            scale1(0, 0)
            dve.wait_ge(s_nmask, 1)
            nc.vector.tensor_scalar(n_valid[:, :], n_masked[:, :], -1.0, float(S), ALU.mult, ALU.add).then_inc(s_nmask, 1)
            nc.vector.tensor_scalar(none_valid[:, :], n_masked[:, :], float(S), None, ALU.is_equal).then_inc(s_nmask, 1)
            dve.wait_ge(s_nmask, 3)
            nc.vector.tensor_scalar(n_valid[:, :], n_valid[:, :], 1.0, None, ALU.max).then_inc(s_cnt, 1)
            dve.wait_ge(s_cnt, 1)
            nc.vector.reciprocal(inv_valid[:, :], n_valid[:, :]).then_inc(s_cnt, 1)
            dve.wait_ge(s_cnt, 2)
            dve.wait_ge(s_const, 16)
            nc.vector.tensor_tensor(
                inv_half[:, :].rearrange("p (t b) -> p t b", b=BPT), inv_valid[:, :].rearrange("p (t b) -> p t b", b=BPT),
                half_mask_sb.rearrange("p (o b) -> p o b", o=1).broadcast_to([P, TILES, BPT]), ALU.mult).then_inc(s_ihalf, 1)
            dve.wait_ge(s_valid, 1)
            nc.vector.tensor_tensor(share_key[:, :], share_key[:, :], none_valid[:, :], ALU.add).then_inc(s_share, 1)
            dve.wait_ge(s_share, 1)
            nc.vector.tensor_tensor(
                share_half[:, :, :], share_key[:, :].rearrange("p (b o) -> p b o", o=1).broadcast_to([P, BATCHES, 2]),
                half_mask_sb.rearrange("p (o e) -> p o e", o=1).broadcast_to([P, BATCHES, 2]),
                ALU.mult).then_inc(s_share, 1)

            for g in range(GROUPS):
                p = g % 2
                if g + 1 < GROUPS:
                    norm1(g + 1, 1 - p)
                dve.wait_ge(s_cmix, g + 1)
                nc.vector.tensor_copy(cmix_sb[p][:, :], cmix_ps[:, :]).then_inc(s_cmix_sb, 1)
                if g + 1 < GROUPS:
                    scale1(g + 1, 1 - p)
                dve.wait_ge(s_v_act, g + 1)
                for b in range(BPT):
                    last = nc.vector.tensor_copy(
                        v_all[S:P, g * GT:(g + 1) * GT, b, :, 0:DK],
                        v_ps[b * S:(b + 1) * S, :].rearrange("p (t j e d) -> p t j e d", t=GT, e=2, d=DK)[:, :, :, 1, :])
                last.then_inc(s_v_dve, 1)
                dve.wait_ge(s_k, g + 1)
                nc.vector.tensor_copy(k_all[:, g * GT:(g + 1) * GT, :, :].rearrange("p t g s -> p g t s"),
                                      k_ps[:, :].rearrange("p (g t s) -> p g t s", g=2, t=GT)).then_inc(s_k_sb, 1)

            dve.wait_ge(s_wproj, 32)

            def step(t, p, on):
                q = 1 - p
                if on(1):
                    dve.wait_ge(s_pv, t)
                    pv = pv_ps[:, 0:HEADS * DV].rearrange("p (h d) -> p h d", d=DV)
                    nc.vector.reciprocal(inv_den[q][:, :], pv[:, :, DK]).then_inc(s_iden, 1)
                    dve.wait_ge(s_iden, t)
                    nc.vector.tensor_tensor(
                        att[q][:, :, :], pv[:, :, 0:DK],
                        inv_den[q][:, :].rearrange("p (h o) -> p h o", o=1).broadcast_to([P, HEADS, DK]),
                        ALU.mult).then_inc(s_att, 1)
                if on(2):
                    dve.wait_ge(s_rstd2, t - 1)
                    nc.vector.tensor_scalar(xn2[p][:, :], x_sb[:, bass.ds(t - 2, 1), :].rearrange("p o d -> p (o d)"),
                                            mv2[p][:, 0:1], rstd2[p][:, :], ALU.subtract, ALU.mult).then_inc(s_xn2, 1)
                if on(-1):
                    dve.wait_ge(s_score, t + 2)
                    for g in range(2):
                        last = nc.vector.tensor_reduce(smax[q][:, g * HG:(g + 1) * HG],
                                                       score_ps[g][:, :].rearrange("p (h s) -> p h s", s=S), AX_X, ALU.max)
                    last.then_inc(s_max, 1)
                    dve.wait_ge(s_max, t + 2)
                    if not (isinstance(t, int) and t < 1):
                        dve.wait_ge(s_pt[1], t)
                    for g in range(2):
                        last = nc.vector.tensor_tensor(
                            prob[q][:, g * GN:(g + 1) * GN].rearrange("p (h s) -> p h s", s=S),
                            score_ps[g][:, :].rearrange("p (h s) -> p h s", s=S),
                            smax[q][:, g * HG:(g + 1) * HG].rearrange("p (h o) -> p h o", o=1).broadcast_to([P, HG, S]),
                            ALU.subtract)
                    last.then_inc(s_sub, 1)
                if on(0):
                    cols = bass.ds(t * W_STEP, W_STEP)
                    dve.wait_ge(s_w_hi, t + 1)
                    nc.vector.tensor_tensor(w_lo[:, cols], w_moe_sb[:, cols], w_hi[:, cols].bitcast(F32),
                                            ALU.subtract).then_inc(s_w_lo, 1)
                if on(1):
                    x1 = x_sb[:, bass.ds(t - 1, 1), :].rearrange("p o d -> p (o d)")
                    dve.wait_ge(s_wo, t)
                    nc.vector.tensor_tensor(x1, x1, wo_ps[:, 0:D], ALU.add).then_inc(s_x1, 1)
                if on(1):
                    dve.wait_ge(s_x1, t)
                    nc.vector.memset(pause[:, q:q + 1], 0.0)
                    nc.vector.bn_stats(stats2[q][:, :], x1).then_inc(s_stat2, 1)
                if on(2):
                    dve.wait_ge(s_logit, t - 1)
                    nc.vector.tensor_tensor(logit[p][:, :], tail_ps[:, 0:EXPERTS], bias_sb[:, :],
                                            ALU.add).then_inc(s_logit_sb, 1)
                if on(1):
                    dve.wait_ge(s_stat2, t)
                    nc.vector.memset(pause[:, 2 + q:3 + q], 0.0)
                    nc.vector.bn_aggr(mv2[q][:, :], stats2[q][:, :]).then_inc(s_mv2, 1)
                if on(2):
                    tile = bass.ds(t - 2, 1)
                    dve.wait_ge(s_logit_sb, t - 1)
                    nc.vector.memset(pause[:, 4 + p:5 + p], 0.0)
                    nc.vector.max(top_v[p][:, :], logit[p][:, :]).then_inc(s_top_v, 1)
                    dve.wait_ge(s_top_v, t - 1)
                    nc.vector.memset(pause[:, 6 + p:7 + p], 0.0)
                    nc.vector.max_index(top_i[p][:, :], top_v[p][:, :], logit[p][:, :]).then_inc(s_top_i, 1)
                    nc.vector.tensor_tensor(gap[:, tile], top_v[p][:, 1:2], top_v[p][:, 0:1], ALU.subtract)
                    dve.wait_ge(s_top_i, t - 1)
                    nc.vector.tensor_copy(top_f[:, tile, :].rearrange("p o k -> p (o k)"),
                                          top_i[p][:, 0:2]).then_inc(s_top_f, 1)
            pipeline(dve, step)

            done = [0]

            def chained(instruction):
                done[0] += 1
                instruction.then_inc(s_route, 1)
                dve.wait_ge(s_route, done[0])

            dve.wait_ge(s_top_f, TILES)
            dve.wait_ge(s_second, 1)
            chained(nc.vector.tensor_scalar(den2[:, :], second[:, :], 1.0, None, ALU.add))
            chained(nc.vector.reciprocal(w_top[:, :, 0], den2[:, :]))
            chained(nc.vector.tensor_tensor(w_top[:, :, 1], second[:, :], w_top[:, :, 0], ALU.mult))
            iota_bc = iota_sb.rearrange("p (o e) -> p o e", o=1).broadcast_to([P, TILES, EXPERTS])
            for k, dst in ((0, comb), (1, comb_b)):
                chained(nc.vector.tensor_tensor(dst[:, :, :], iota_bc,
                                                top_f[:, :, k:k + 1].broadcast_to([P, TILES, EXPERTS]), ALU.is_equal))
                chained(nc.vector.tensor_tensor(dst[:, :, :], dst[:, :, :],
                                                w_top[:, :, k:k + 1].broadcast_to([P, TILES, EXPERTS]), ALU.mult))
            chained(nc.vector.tensor_tensor(comb[:, :, :], comb[:, :, :], comb_b[:, :, :], ALU.add))
            for part in range(PARTS):
                chained(nc.vector.tensor_copy(comb3[:, :, part, :], comb[:, :, :]))
                if part < PARTS - 1:
                    chained(nc.vector.tensor_tensor(comb[:, :, :], comb[:, :, :], comb3[:, :, part, :], ALU.subtract))
            nc.vector.tensor_copy(top_f[:, 0, 0:1], top_f[:, 0, 0:1]).then_inc(s_comb3, 1)

            def result(i, half):
                g = i * 2 + half
                rows = x_sb[:, bass.ds(g * GT, GT), :]
                dve.wait_ge(s_yt, g + 1)
                nc.vector.tensor_tensor(rows, yt_ps[:, :].rearrange("p (t d) -> p t d", d=D), rows,
                                        ALU.add).then_inc(s_y, 1)

            def body(i):
                for m in range(BODY + 1):
                    n, r = i * BODY + m, m % 2
                    if m < BODY:
                        g, u = group_of(i, m)
                        routed = u < EPAIRS
                        dve.wait_ge(s_sig, n + 1)
                        dve.wait_ge(s_up, n + 1)
                        if m >= 2 and not routed:
                            dve.wait_ge(s_hid_lo, n - 1)
                        dst = hid_u[r] if routed else hid[r]
                        nc.vector.tensor_tensor(dst[:, :], sig[r][:, :], up_ps[r][:, :], ALU.mult)\
                            .then_inc(s_hid_u, 1)
                        if routed:
                            dve.wait_ge(s_hid_u, n + 1)
                            dve.wait_ge(s_cb, g * EPAIRS + u + 1)
                            if m >= 2:
                                dve.wait_ge(s_hid_lo, n - 1)
                            nc.vector.tensor_tensor(hid[r][:, :], hid_u[r][:, :], cb_ps[r][:, :], ALU.mult).then_inc(s_hid, 1)
                    if m >= 1:
                        q = 1 - r
                        dve.wait_ge(s_hid_hi, n)
                        if m >= 3:
                            dve.wait_ge(s_down, n - 2)
                        nc.vector.tensor_tensor(hid_lo[q][:, :], hid[q][:, :], hid_hi[q][:, :].bitcast(F32),
                                                ALU.subtract).then_inc(s_hid_lo, 1)
                    if m == UNITS + 3:
                        result(i, 0)
                result(i, 1)
            expert_bodies(dve, body)

        @block.tensor
        def _(pe):
            pe.wait_ge(s_const, 16)

            def project(g, p, first=False):
                pe.wait_ge(s_xn, g + 1)
                if not first:
                    pe.wait_ge(s_xt_sb, g)
                for i in range(GT):
                    last = nc.tensor.transpose(xt_ps[:, i * P:(i + 1) * P], xn[p][:, i, :], ident_sb)
                last.then_inc(s_xt, 1)
                if first:
                    pe.wait_ge(s_wproj, 32)
                pe.wait_ge(s_ctxv, g + 1)
                pe.wait_ge(s_mix, g + 1)
                if not first:
                    pe.wait_ge(s_cmix_sb, g)
                for i in range(GT):
                    last = nc.tensor.matmul(cmix_ps[:, i * P:(i + 1) * P], ctxv_sb[p][:, i, :], mix_all[:, g * GT + i, :],
                                            start=True, stop=True)
                last.then_inc(s_cmix, 1)
                pe.wait_ge(s_ctxt[p], 16 * (g // 2 + 1))
                if not first:
                    pe.wait_ge(s_v_act, g)
                    pe.wait_ge(s_v_dve, g)
                for i in range(GT):
                    last = nc.tensor.matmul(v_ps[:, i * P:(i + 1) * P], ctxt_sb[p][:, i * P:(i + 1) * P], wv_sb,
                                            start=True, stop=True)
                last.then_inc(s_v, 1)
                for w, src, have, dst, drained, made in ((wq_sb, xt_sb, s_xt_sb, q_ps, s_q_sb, s_q),
                                                        (wk_sb, cmix_sb, s_cmix_sb, k_ps, s_k_sb, s_k)):
                    pe.wait_ge(have, g + 1)
                    if not first:
                        pe.wait_ge(drained, g)
                    for hg in range(2):
                        for b in range(BPT):
                            last = nc.tensor.matmul(
                                dst[b * ROWS:(b + 1) * ROWS, hg * GT * S:(hg + 1) * GT * S],
                                w[:, hg * ROWS:(hg + 1) * ROWS],
                                src[p][:, :].rearrange("p (t b s) -> p t b s", b=BPT, s=S)[:, :, b, :],
                                start=True, stop=True)
                    last.then_inc(made, 1)
            for g in range(GROUPS):
                project(g, g % 2, first=g == 0)

            def step(t, p, on):
                q = 1 - p

                def transposes(h):
                    if not (isinstance(t, int) and t < 1):
                        pe.wait_ge(s_pt_sb[h], t)
                    for j in range(GT):
                        c = (h * GT + j) * P
                        last = nc.tensor.transpose(pt_ps[h][:, j * P:(j + 1) * P], prob[p][:, c:c + P], ident_sb)
                    last.then_inc(s_pt[h], 1)

                def values(b):
                    rows = slice(b * S, (b + 1) * S)
                    for j in range(PAIRS):
                        last = nc.tensor.matmul(
                            pv_ps[rows, j * 2 * DV:(j + 1) * 2 * DV], prob_t[p][:, j, b * S:(b + 1) * S],
                            v_blk[p][:, b, j, :, :].rearrange("p e d -> p (e d)"), start=True, stop=True)
                    return last

                if on(-1):
                    pe.wait_ge(s_blk, t + 2)
                    if not (isinstance(t, int) and t < 0):
                        pe.wait_ge(s_sub, t + 1)
                    for g in range(2):
                        last = nc.tensor.matmul(score_ps[g][:, :], q_blk[q][:, g, :, :].rearrange("p b s -> p (b s)"),
                                                k_blk[q][:, g, :, :].rearrange("p h s -> p (h s)"), start=True, stop=True)
                    last.then_inc(s_score, 1)
                if on(1):
                    pe.wait_ge(s_att, t)
                    if not (isinstance(t, int) and t < 2):
                        pe.wait_ge(s_at_sb, t - 1)
                    nc.tensor.transpose(at_ps[:, 0:P], att[q][:, :, :].rearrange("p h d -> p (h d)"),
                                        ident_sb).then_inc(s_at, 1)
                if on(0):
                    pe.wait_ge(s_exp, t + 1)
                    transposes(0)
                if on(1):
                    pe.wait_ge(s_at_sb, t)
                    if not (isinstance(t, int) and t < 2):
                        pe.wait_ge(s_x1, t - 1)
                    nc.tensor.matmul(wo_ps[:, 0:D], att_t[q][:, :], wo_sb, start=True, stop=True).then_inc(s_wo, 1)
                if on(0):
                    transposes(1)
                if on(2):
                    pe.wait_ge(s_xn2, t - 1)
                    if not (isinstance(t, int) and t < 3):
                        pe.wait_ge(s_logit_sb, t - 2)
                    nc.tensor.transpose(tail_ps[:, 0:P], xn2[p][:, :], ident_sb).then_inc(s_xt2, 1)
                if on(0):
                    pe.wait_ge(s_vblk, t + 1)
                    for h in range(2):
                        pe.wait_ge(s_pt_sb[h], t + 1)
                    if not (isinstance(t, int) and t < 1):
                        pe.wait_ge(s_att, t)
                    values(0)
                if on(2):
                    pe.wait_ge(s_xt2_sb, t - 1)
                    pe.wait_ge(s_xt2_hi, t - 1)
                    nc.tensor.matmul(tail_ps[:, 0:EXPERTS], xt2[p][:, :], wr_sb, start=True,
                                     stop=True).then_inc(s_logit, 1)
                if on(0):
                    values(1).then_inc(s_pv, 1)
            pipeline(pe, step)

            pe.wait_ge(s_comb3, 1)
            for g in range(GROUPS):
                for i in range(GT):
                    last = nc.tensor.transpose(bank_bf16(banks[g])[0:PARTS * EXPERTS, i * P:(i + 1) * P],
                                               comb3[:, g * GT + i, :, :].rearrange("p k e -> p (k e)"), identb_sb[:, :])
                last.then_inc(s_ct, 1)

            pe.wait_ge(s_xt2_lo, TILES)
            pe.wait_ge(s_w_lo, TILES)
            pe.wait_ge(s_ct_sb, GROUPS)

            def three_products(out, w_parts, moving_parts, start, stop):
                (wh, wl), (mh, ml) = w_parts, moving_parts
                for k, (w, moving) in enumerate(((wh, mh), (wh, ml), (wl, mh))):
                    last = nc.tensor.matmul(out, w, moving, start=start and k == 0, stop=stop and k == 2)
                return last

            def body(i):
                def transpose_sums(half):
                    for k in range(GT):
                        last = nc.tensor.transpose(yt_ps[:, k * P:(k + 1) * P], moe_t[half][:, k * P:(k + 1) * P], ident_sb)
                    last.then_inc(s_yt, 1)

                for m in range(BODY + 2):
                    n, r = i * BODY + m, m % 2
                    if m < BODY:
                        g, u = group_of(i, m)
                        cols = bass.ds(g * GN, GN)
                        x_parts = (xt2_hi[:, cols], xt2_lo[:, cols])
                        if m >= 2:
                            pe.wait_ge(s_sig, n - 1)
                        three_products(gate_ps[r][:, :], (w_slice(w_hi, u, 0), w_slice(w_lo, u, 0)), x_parts,
                                       True, True).then_inc(s_gate, 1)
                        if m >= 2:
                            pe.wait_ge(s_hid_u, n - 1)
                            if u < EPAIRS:
                                wait_hid(pe, i, m - 2)
                        three_products(up_ps[r][:, :], (w_slice(w_hi, u, 1), w_slice(w_lo, u, 1)), x_parts,
                                       True, True).then_inc(s_up, 1)
                        if u < EPAIRS:
                            nc.tensor.matmul(cb_ps[r][:, :], sel_sb[:, u, :], comb_t[:, cols], start=True,
                                             stop=True).then_inc(s_cb, 1)
                    if m >= 2:
                        _, u = group_of(i, m - 2)
                        if m - 2 == UNITS:
                            pe.wait_ge(s_moe_sb, i * 2 + 1)
                        pe.wait_ge(s_hid_lo, n - 1)
                        three_products(moe_ps[:, :], (w_slice(w_hi, u, 2), w_slice(w_lo, u, 2)),
                                       (hid_hi[r][:, :], hid_lo[r][:, :]), u == 0, u == UNITS - 1).then_inc(s_down, 1)
                        if m - 2 == UNITS:
                            transpose_sums(0)
                pe.wait_ge(s_moe_sb, i * 2 + 2)
                pe.wait_ge(s_y, i * 2 + 1)
                transpose_sums(1)
            expert_bodies(pe, body)


def host_layout(inputs):
    a = {k: np.asarray(v) for k, v in inputs.items()}
    c = np.ascontiguousarray
    mask = a["mask_Bx1x1xS2_bk0"].reshape(TOKENS)
    key_rows = mask.reshape(BATCHES, S).T
    ctx = a["ctx_1024"].reshape(TOKENS, D)

    def pairs(w):
        return w.transpose(1, 0, 2).reshape(D, EPAIRS, P)

    gate = np.concatenate([pairs(a["L0_ffn_gate_proj"]), a["L0_ffn_sh_gate"].T[:, None, :]], axis=1)
    up = np.concatenate([pairs(a["L0_ffn_up_proj"]), a["L0_ffn_sh_up"].T[:, None, :]], axis=1)
    down = np.concatenate([a["L0_ffn_down_proj"].reshape(EPAIRS, P, D).transpose(1, 0, 2),
                           a["L0_ffn_sh_down"].T[:, None, :]], axis=1)
    w_moe = np.stack([gate, up, down], axis=2).reshape(P, W_MOE)
    w_att = np.concatenate([a["L0_xattn_" + w].T for w in ("Wq", "Wk", "Wv", "Wo")] + [a["L0_ffn_router_w"].T], axis=1)
    ident = np.eye(P, dtype=np.float32)
    head_of_row = (np.arange(P) % ROWS) // DK
    head_mask = (head_of_row[:, None] == np.arange(HG)[None, :]).astype(np.float32)
    expert_of_row = np.arange(PARTS * EXPERTS) % EXPERTS
    expert_of_col = (2 * np.arange(EPAIRS)[:, None] + np.arange(P)[None, :] // E_DIM)
    sel = expert_of_row[:, None, None] == expert_of_col[None]
    bf16 = mybir.dt.np(BF16)
    half_mask = (np.arange(P)[:, None] // S == np.arange(2)[None, :]).astype(np.float32)
    iota = np.tile(np.arange(EXPERTS, dtype=np.float32), (P, 1))
    return {
        "x": c(a["x"].reshape(TOKENS, D)), "ctx_nat": c(ctx), "ctx_t": c(ctx.T),
        "mask_row": c(mask.reshape(1, TOKENS)),
        "mask_col": c(np.concatenate([mask.reshape(TILES, P).T, np.concatenate([key_rows, key_rows], axis=0)], axis=1)),
        "w_att": c(w_att), "router_bias": c(a["L0_ffn_router_bias"].reshape(1, EXPERTS)), "w_moe": c(w_moe),
        "consts": c(np.concatenate([ident, head_mask, half_mask, iota], axis=1)),
        "ident_bf": ident.astype(bf16), "expert_sel": sel.astype(bf16),
    }


def kernel(**inputs):
    import concourse.bacc as bacc
    from concourse.bass_utils import run_bass_kernel_spmd

    nc = bacc.Bacc("TRN2", target_bir_lowering=False, num_devices=1)
    arrays = host_layout(inputs)
    args = {n: nc.dram_tensor(n, a.shape, mybir.dt.from_np(a.dtype), kind="ExternalInput").ap()
            for n, a in arrays.items()}
    out = nc.dram_tensor("out", (TOKENS, D), F32, kind="ExternalOutput").ap()
    build_program(nc, out=out, **args)
    r = run_bass_kernel_spmd(nc, [arrays], core_ids=[0])
    return r.results[0]["out"].reshape(BATCHES, S, D)
```

```python
from contextlib import ExitStack

import numpy as np

import concourse.bass as bass
from concourse import mybir

F32 = mybir.dt.float32
F32R = mybir.dt.float32r
BF16 = mybir.dt.bfloat16
U8 = mybir.dt.uint8
U32 = mybir.dt.uint32
ALU = mybir.AluOpType
ACT = mybir.ActivationFunctionType
AX_X = mybir.AxisListType.X

P = 128
BATCHES, S, D = 32, 64, 128
HEADS, DK = 16, 8
TOKENS = BATCHES * S
TILES = TOKENS // P
BPT = P // S
HG = HEADS // 2
ROWS = HG * DK
PAIRS = HEADS // 2
DV = DK + 1
PW = 32
EXPERTS, E_DIM = 16, 64
EPAIRS = EXPERTS // 2
UNITS = EPAIRS + 1
GT = 4
GROUPS = TILES // GT
GN = GT * P
PARTS = 3
LN_EPS = 1e-5
W_MOE = 3 * UNITS * P
W_UNIT = 3 * P
W_STEP = W_MOE // TILES
SCORE_SCALE = float(DK) ** 0.5


def build_program(nc, x, ctx_nat, ctx_t, mask_row, mask_col, w_att, router_bias, w_moe, consts, ident_bf,
                  expert_sel, out):
    stack = ExitStack()
    with stack:
        def sb(name, shape, dt=F32):
            return stack.enter_context(nc.sbuf_tensor(name, shape, dt))

        def sem(name):
            return stack.enter_context(nc.semaphore(name))

        consts_sb = sb("consts_sb", [P, P + HG + 2 + EXPERTS])
        ident_sb = consts_sb[:, 0:P]
        hmask_sb = consts_sb[:, P:P + HG]
        half_mask_sb = consts_sb[:, P + HG:P + HG + 2]
        iota_sb = consts_sb[:, P + HG + 2:]
        identb_sb = sb("identb_sb", [P, P], BF16)
        bias_sb = sb("bias_sb", [P, EXPERTS])
        sel_sb = sb("sel_sb", [PARTS * EXPERTS, EPAIRS, P], BF16)
        w_att_sb = sb("w_att_sb", [P, 4 * D + EXPERTS])
        wq_sb, wk_sb, wv_sb, wo_sb = (w_att_sb[:, i * D:(i + 1) * D] for i in range(4))
        wr_sb = w_att_sb[:, 4 * D:]
        w_moe_sb = sb("w_moe_sb", [P, W_MOE])
        w_hi = sb("w_hi", [P, W_MOE], F32R)
        w_lo = sb("w_lo", [P, W_MOE], F32R)
        x_sb = sb("x_sb", [P, TILES, D])
        q_all = sb("q_all", [P, TILES, 2, S])
        k_all = sb("k_all", [P, TILES, 2, S])
        v_all = sb("v_all", [P, TILES, BPT, PAIRS, 2, DV])
        mix_all = sb("mix_all", [P, TILES, P])
        xt2_hi = sb("xt2_hi", [P, TOKENS], F32R)
        xt2_lo = sb("xt2_lo", [P, TOKENS], F32R)
        comb_t = sb("comb_t", [PARTS * EXPERTS, TOKENS], BF16)
        mrow8 = sb("mrow8", [P, TOKENS], U8)
        mcol8 = sb("mcol8", [P, TILES + BATCHES], U8)
        valid_col = sb("valid_col", [P, TILES])
        share_key = sb("share_key", [P, BATCHES])
        valid_key = sb("valid_key", [P, BATCHES])
        half_sb = sb("half_sb", [P, P])
        n_valid = sb("n_valid", [P, BATCHES])
        inv_valid = sb("inv_valid", [P, BATCHES])
        inv_half = sb("inv_half", [P, BATCHES])
        none_valid = sb("none_valid", [P, BATCHES])
        xn = [sb(f"xn{p}", [P, GT, D]) for p in range(2)]
        ctx_sb = [sb(f"ctx_sb{p}", [P, GT, D]) for p in range(2)]
        ctxv_sb = [sb(f"ctxv_sb{p}", [P, GT, D]) for p in range(2)]
        ctxt_sb = [sb(f"ctxt_sb{p}", [P, GN]) for p in range(2)]
        xt_sb = [sb(f"xt_sb{p}", [P, GN]) for p in range(2)]
        cmix_sb = [sb(f"cmix_sb{p}", [P, GN]) for p in range(2)]
        stats1 = [sb(f"stats1_{p}", [P, GT, 6]) for p in range(2)]
        mv1 = [sb(f"mv1_{p}", [P, GT, 2]) for p in range(2)]
        rstd1 = [sb(f"rstd1_{p}", [P, GT]) for p in range(2)]
        veps1 = [sb(f"veps1_{p}", [P, GT]) for p in range(2)]
        neg_half = sb("neg_half", [P, GT])
        eps_sb = sb("eps_sb", [P, GT])
        pause = sb("pause", [P, 8])
        q_blk = [sb(f"q_blk{p}", [P, 2, BPT, S]) for p in range(2)]
        k_blk = [sb(f"k_blk{p}", [P, 2, HG, S]) for p in range(2)]
        v_blk = [sb(f"v_blk{p}", [P, BPT, PAIRS, PW]) for p in range(2)]
        pvt_sb = sb("pvt_sb", [P, 2 * P])
        smax = [sb(f"smax{p}", [P, HEADS]) for p in range(2)]
        prob = [sb(f"prob{p}", [P, HEADS * S]) for p in range(2)]
        prob_t = [sb(f"prob_t{p}", [P, PAIRS, P]) for p in range(2)]
        inv_den = [sb(f"inv_den{p}", [P, HEADS]) for p in range(2)]
        att = [sb(f"att{p}", [P, HEADS, DK]) for p in range(2)]
        att_t = [sb(f"att_t{p}", [P, P]) for p in range(2)]
        stats2 = [sb(f"stats2_{p}", [P, 6]) for p in range(2)]
        mv2 = [sb(f"mv2_{p}", [P, 2]) for p in range(2)]
        veps2 = [sb(f"veps2_{p}", [P, 1]) for p in range(2)]
        neg_mean2 = [sb(f"neg_mean2_{p}", [P, 1]) for p in range(2)]
        bias2 = [sb(f"bias2_{p}", [P, 1]) for p in range(2)]
        rstd2 = [sb(f"rstd2_{p}", [P, 1]) for p in range(2)]
        xn2 = [sb(f"xn2_{p}", [P, D]) for p in range(2)]
        xt2 = [sb(f"xt2_{p}", [P, P]) for p in range(2)]
        logit = [sb(f"logit{p}", [P, EXPERTS]) for p in range(2)]
        top_v = [sb(f"top_v{p}", [P, 8]) for p in range(2)]
        top_i = [sb(f"top_i{p}", [P, 8], U32) for p in range(2)]
        top_f = sb("top_f", [P, TILES, 2])
        gap = sb("gap", [P, TILES])
        half_tanh = sb("half_tanh", [P, TILES])
        w_top = sb("w_top", [P, TILES, 2])
        comb = sb("comb", [P, TILES, EXPERTS])
        comb_b = sb("comb_b", [P, TILES, EXPERTS])
        comb3 = sb("comb3", [P, TILES // 2, PARTS, EXPERTS], BF16)
        sig = [sb(f"sig{p}", [P, GN]) for p in range(2)]
        hid_u = [sb(f"hid_u{p}", [P, GN]) for p in range(2)]
        hid = [sb(f"hid{k}", [P, GN]) for k in range(2)] + [cmix_sb[1]]
        hid_hi = [sb(f"hid_hi{k}", [P, GN], F32R) for k in range(3)]
        hid_lo = [sb(f"hid_lo{k}", [P, GN], F32R) for k in range(3)]
        moe_t = cmix_sb[0]

        banks = [stack.enter_context(nc.psum_tensor(f"bank{i}", [P, GN], F32)) for i in range(8)]

        s_x = [sem(f"s_xload{g}") for g in range(GROUPS)]
        s_const = sem("s_const")
        s_mask_col = sem("s_mask_col")
        s_mask_row = sem("s_mask_row")
        s_wproj = sem("s_wproj")
        s_wmoe = sem("s_wmoe")
        s_ctx = [sem(f"s_ctx{p}") for p in range(2)]
        s_ctxt = [sem(f"s_ctxt{p}") for p in range(2)]
        s_valid = sem("s_valid")
        s_nvalid = sem("s_nvalid")
        s_cnt = sem("s_cnt")
        s_ihalf = sem("s_ihalf")
        s_vcol = sem("s_vcol")
        s_ctxv = sem("s_ctxv")
        s_mrow = sem("s_mrow")
        s_mean = sem("s_mean")
        s_mix = sem("s_mix")
        s_zero = [sem(f"s_zero{h}") for h in range(2)]
        s_half = sem("s_half")
        s_share = sem("s_share")
        s_vden = sem("s_vden")
        s_stat1 = sem("s_stat1")
        s_mv1 = sem("s_mv1")
        s_veps1 = sem("s_veps1")
        s_rstd1 = sem("s_rstd1")
        s_xn = sem("s_xn")
        s_xt = sem("s_xt")
        s_xt_sb = sem("s_xt_sb")
        s_cmix = sem("s_cmix")
        s_cmix_sb = sem("s_cmix_sb")
        s_v = sem("s_v")
        s_v_sb = sem("s_v_sb")
        s_q = sem("s_q")
        s_q_sb = sem("s_q_sb")
        s_k = sem("s_k")
        s_k_sb = sem("s_k_sb")
        s_blk = sem("s_blk")
        s_vblk = sem("s_vblk")
        s_score = [sem(f"s_score{g}") for g in range(2)]
        s_max = [sem(f"s_max{g}") for g in range(2)]
        s_sub = [sem(f"s_sub{g}") for g in range(2)]
        s_exp = [sem(f"s_exp{g}") for g in range(2)]
        s_pt = [sem(f"s_pt{h}") for h in range(2)]
        s_pt_sb = [sem(f"s_pt_sb{h}") for h in range(2)]
        s_pvt = sem("s_pvt")
        s_pvt_sb = sem("s_pvt_sb")
        s_pv = sem("s_pv")
        s_vwide = sem("s_vwide")
        s_iden = sem("s_iden")
        s_att = sem("s_att")
        s_at = sem("s_at")
        s_at_sb = sem("s_at_sb")
        s_wo = sem("s_wo")
        s_x1 = sem("s_x1")
        s_stat2 = sem("s_stat2")
        s_mv2 = sem("s_mv2")
        s_veps2 = sem("s_veps2")
        s_rstd2 = sem("s_rstd2")
        s_nmean2 = sem("s_nmean2")
        s_bias2 = sem("s_bias2")
        s_xn2 = sem("s_xn2")
        s_xt2 = sem("s_xt2")
        s_xt2_hi = sem("s_xt2_hi")
        s_xt2_lo = sem("s_xt2_lo")
        s_w_hi = sem("s_w_hi")
        s_w_lo = sem("s_w_lo")
        s_logit = sem("s_logit")
        s_logit_sb = sem("s_logit_sb")
        s_top_v = sem("s_top_v")
        s_top_i = sem("s_top_i")
        s_top_f = sem("s_top_f")
        s_route = [sem(f"s_route{h}") for h in range(2)]
        s_tanh = sem("s_tanh")
        s_w_top = sem("s_w_top")
        s_comb3 = sem("s_comb3")
        s_ct = sem("s_ct")
        s_ct_sb = sem("s_ct_sb")
        s_gate = sem("s_gate")
        s_up = sem("s_up")
        s_cb = sem("s_cb")
        s_sig = sem("s_sig")
        s_hid_u = sem("s_hid_u")
        s_hid = sem("s_hid")
        s_hid_hi = sem("s_hid_hi")
        s_hid_lo = sem("s_hid_lo")
        s_down = sem("s_down")
        s_moe_sb = sem("s_moe_sb")
        s_yt = sem("s_yt")
        s_y = sem("s_y")
        s_out = [sem(f"s_out{p}") for p in range(2)]

        x_view = x.rearrange("(t p) d -> p t d", p=P)
        ctx_view = ctx_nat.rearrange("(t p) d -> p t d", p=P)
        out_view = out.rearrange("(t p) d -> p t d", p=P)

        xt_ps, cmix_ps, v_ps, q_ps, k_ps = banks[0:5]
        count_ps = banks[7]
        score_ps = banks[5:7]
        pt_ps = [banks[7], banks[0]]
        pvt_ps = banks[1][:, 0:2 * P]
        pv_ps = banks[1][:, 2 * P:]
        at_ps, wo_ps, tail_ps = (bank[:, 0:P] for bank in banks[2:5])
        gate_ps = banks[5:7]
        up_ps = [banks[7], banks[0]]
        cb_ps = banks[1:3]
        moe_ps = banks[3]
        yt_ps = banks[4]

        def bank_bf16(bank):
            return bank[:, :].bitcast(BF16)

        def paired_loop(eng, first, last, step):
            assert (last - first) % 2 == 0
            with eng.Fori(0, (last - first) // 2) as i:
                for parity in range(2):
                    step(i * 2 + (first + parity), (first + parity) % 2)

        LEAD, TRAIL = -1, 3

        def peel(step, t):
            step(t, t % 2, lambda lag: 0 <= t - lag < TILES)

        def pipeline(eng, step):
            start, end = TRAIL + 1, TILES - 2
            for t in range(LEAD + 1, start):
                peel(step, t)
            with eng.Fori(0, (end - start) // 2) as i:
                for parity in range(2):
                    step(i * 2 + (start + parity), (start + parity) % 2, lambda lag: True)
            for t in range(end, TILES):
                peel(step, t)

        def expert_slots(eng, slot, first):
            for m in range(first, UNITS):
                slot(0, m)
            with eng.Fori(0, GROUPS - 1) as i:
                for m in range(UNITS):
                    slot(i + 1, m)
            for m in range(2):
                slot(GROUPS, m)

        def exists(g, m, back=0):
            n = g * UNITS + m - back if isinstance(g, int) else 0
            return 0 <= n < GROUPS * UNITS

        def back_to_buffer(m):
            return {0: 1, 1: 3}.get(m, 2)

        def wait_hid(eng, g, m):
            if m == 0:
                eng.wait_ge(s_hid_u, g * UNITS + 1)
            elif m > 0:
                eng.wait_ge(s_hid, g * EPAIRS + m)
            else:
                eng.wait_ge(s_hid, g * EPAIRS + (m + 1))

        def expert_weights(eng, ops, half, written):
            tiles = slice(half * TILES // 2, (half + 1) * TILES // 2)
            shape = [P, TILES // 2, EXPERTS]
            eng.wait_ge(s_w_top, half + 1)
            for k, dst in ((0, comb), (1, comb_b)):
                last = ops.tensor_tensor(dst[:, tiles, :], dst[:, tiles, :], w_top[:, tiles, k:k + 1].broadcast_to(shape),
                                         ALU.mult)
            last.then_inc(written, 1)
            eng.wait_ge(written, 1)
            ops.tensor_tensor(comb[:, tiles, :], comb[:, tiles, :], comb_b[:, tiles, :], ALU.add).then_inc(written, 1)
            eng.wait_ge(written, 2)
            if half == 1:
                eng.wait_ge(s_ct, 1)
            for part in range(PARTS - 1):
                ops.tensor_copy(comb3[:, :, part, :], comb[:, tiles, :]).then_inc(written, 1)
                eng.wait_ge(written, 3 + 2 * part)
                ops.tensor_tensor(comb[:, tiles, :], comb[:, tiles, :], comb3[:, :, part, :],
                                  ALU.subtract).then_inc(written, 1)
                eng.wait_ge(written, 4 + 2 * part)
            ops.tensor_copy(comb3[:, :, PARTS - 1, :], comb[:, tiles, :]).then_inc(s_comb3, 1)

        def w_slice(w, u, kind):
            c = (3 * u + kind) * P
            return w[:, c:c + P]

        block = stack.enter_context(nc.Block())

        @block.sync
        def _(sp):
            sp.dma_start(x_sb[:, 0:GT, :], x_view[:, 0:GT, :]).then_inc(s_x[0], 16)
            sp.dma_start(consts_sb[:, :], consts).then_inc(s_const, 16)
            for p in range(2):
                sp.dma_start(ctx_sb[p][:, :, :], ctx_view[:, p * GT:(p + 1) * GT, :]).then_inc(s_ctx[p], 16)
                sp.dma_start(ctxt_sb[p][:, :], ctx_t[:, p * GN:(p + 1) * GN]).then_inc(s_ctxt[p], 16)
                sp.dma_start(x_sb[:, (p + 1) * GT:(p + 2) * GT, :], x_view[:, (p + 1) * GT:(p + 2) * GT, :]).then_inc(s_x[p + 1], 16)
            sp.dma_start(x_sb[:, 3 * GT:, :], x_view[:, 3 * GT:, :]).then_inc(s_x[3], 16)
            for p in range(2):
                g = p + 2
                sp.wait_ge(s_ctxv, g - 1)
                sp.dma_start(ctx_sb[p][:, :, :], ctx_view[:, g * GT:(g + 1) * GT, :]).then_inc(s_ctx[p], 16)
                sp.wait_ge(s_v, g - 1)
                sp.dma_start(ctxt_sb[p][:, :], ctx_t[:, g * GN:(g + 1) * GN]).then_inc(s_ctxt[p], 16)
            sp.dma_start(w_moe_sb[:, :], w_moe).then_inc(s_wmoe, 16)
            sp.dma_start(sel_sb[:, :, :], expert_sel).then_inc(s_wmoe, 16)
            sp.dma_start(identb_sb[:, :], ident_bf).then_inc(s_wmoe, 16)
            def store(g, p):
                sp.wait_ge(s_y, g + 1)
                sp.dma_start(out_view[:, bass.ds(g * GT, GT), :], x_sb[:, bass.ds(g * GT, GT), :]).then_inc(s_out[p], 16)
            paired_loop(sp, 0, GROUPS, store)
            for p in range(2):
                sp.wait_ge(s_out[p], 16 * GROUPS // 2)

        @block.gpsimd
        def _(pool):
            nc.gpsimd.memset(half_sb[:, :], 0.5).then_inc(s_half, 1)
            nc.gpsimd.memset(neg_half[:, :], -0.5).then_inc(s_half, 1)
            nc.gpsimd.memset(eps_sb[:, :], LN_EPS).then_inc(s_half, 1)
            for p in range(2):
                nc.gpsimd.memset(v_blk[p][:, :, :, :].rearrange("p b j w -> p (b j w)"), 0.0).then_inc(s_vwide, 1)
            nc.gpsimd.memset(v_all[:, TILES // 2:, :, :, :, :].rearrange("p t b j e d -> p (t b j e d)"), 0.0)\
                .then_inc(s_zero[1], 1)
            pool.wait_ge(s_half, 3)

            def rstd1_of(g):
                p = g % 2
                pool.wait_ge(s_mv1, g + 1)
                nc.gpsimd.tensor_tensor(veps1[p][:, :], mv1[p][:, :, 1], eps_sb[:, :], ALU.add).then_inc(s_veps1, 1)
                pool.wait_ge(s_veps1, g + 1)
                nc.gpsimd.tensor_tensor(rstd1[p][:, :], veps1[p][:, :], neg_half[:, :], ALU.pow).then_inc(s_rstd1, 1)

            def mix_of(g):
                mix = mix_all[:, g * GT:(g + 1) * GT, :]
                blk = mix.rearrange("p t (b s) -> p (t b) s", b=BPT)
                pool.wait_ge(s_mrow, g + 1)
                nc.gpsimd.tensor_tensor(
                    blk, blk,
                    inv_half[:, g * GT * BPT:(g + 1) * GT * BPT].rearrange("p (b o) -> p b o", o=1)
                    .broadcast_to([P, GT * BPT, S]), ALU.mult).then_inc(s_mean, 1)
                pool.wait_ge(s_mean, g + 1)
                nc.gpsimd.tensor_tensor(mix, mix, ident_sb.rearrange("p (o s) -> p o s", o=1).broadcast_to([P, GT, P]),
                                        ALU.add).then_inc(s_mix, 1)

            def q_block(t, p, first):
                if not first:
                    pool.wait_ge(s_score[1], t - 1)
                nc.gpsimd.tensor_tensor(
                    q_blk[p][:, :, :, :],
                    q_all[:, bass.ds(t, 1), :, :].rearrange("p o g (c s) -> p (o g) c s", c=1).broadcast_to([P, 2, BPT, S]),
                    half_mask_sb.rearrange("p (o b e) -> p o b e", o=1, e=1).broadcast_to([P, 2, BPT, S]), ALU.mult)

            def k_blocks(t, p):
                for g in range(2):
                    last = nc.gpsimd.tensor_tensor(
                        k_blk[p][:, g, :, :],
                        k_all[:, bass.ds(t, 1), g, :].broadcast_to([P, HG, S]),
                        hmask_sb.rearrange("p (h o) -> p h o", o=1).broadcast_to([P, HG, S]), ALU.mult)
                last.then_inc(s_blk, 1)

            rstd1_of(0)
            pool.wait_ge(s_const, 16)
            pool.wait_ge(s_ihalf, 1)
            for g in range(GROUPS):
                mix_of(g)
                if g == GROUPS - 2:
                    pool.wait_ge(s_q_sb, 1)
                    pool.wait_ge(s_k_sb, 1)
                    q_block(0, 0, first=True)
                    k_blocks(0, 0)
                if g + 1 < GROUPS:
                    rstd1_of(g + 1)
            q_block(1, 1, first=True)
            k_blocks(1, 1)
            pool.wait_ge(s_q_sb, GROUPS)
            pool.wait_ge(s_k_sb, GROUPS)

            LOW_WEIGHTS = ((0, 1, 2), (3, 4), (5, 6), (7, 8))

            def low_weights(u):
                cols = slice(u * W_UNIT, (u + 1) * W_UNIT)
                pool.wait_ge(s_w_hi, min(TILES, -(-(u + 1) * W_UNIT // W_STEP)))
                nc.gpsimd.tensor_tensor(w_lo[:, cols], w_moe_sb[:, cols], w_hi[:, cols].bitcast(F32),
                                        ALU.subtract).then_inc(s_w_lo, 1)

            def step(t, p, on):
                if on(-2):
                    q_block(t + 2, p, first=False)
                if on(2):
                    pool.wait_ge(s_mv2, t - 1)
                    nc.gpsimd.tensor_tensor(veps2[p][:, :], mv2[p][:, 1:2], eps_sb[:, 0:1], ALU.add).then_inc(s_veps2, 1)
                    pool.wait_ge(s_veps2, t - 1)
                    nc.gpsimd.tensor_tensor(rstd2[p][:, :], veps2[p][:, :], neg_half[:, 0:1],
                                            ALU.pow).then_inc(s_rstd2, 1)
                    pool.wait_ge(s_rstd2, t - 1)
                    pool.wait_ge(s_nmean2, t - 1)
                    nc.gpsimd.tensor_tensor(bias2[p][:, :], neg_mean2[p][:, :], rstd2[p][:, :], ALU.mult).then_inc(s_bias2, 1)
                if on(-2):
                    k_blocks(t + 2, p)
                elif t - (TILES - 2) < len(LOW_WEIGHTS):
                    for u in LOW_WEIGHTS[t - (TILES - 2)]:
                        low_weights(u)
                if on(2):
                    cols = bass.ds((t - 2) * P, P)
                    pool.wait_ge(s_xt2_hi, t - 1)
                    nc.gpsimd.tensor_tensor(xt2_lo[:, cols], xt2[p][:, :], xt2_hi[:, cols].bitcast(F32),
                                            ALU.subtract).then_inc(s_xt2_lo, 1)
            pipeline(pool, step)
            for t in range(TILES, TILES + TRAIL):
                peel(step, t)

            expert_weights(pool, nc.gpsimd, 1, s_route[1])

        @block.scalar
        def _(act):
            act.dma_start(mcol8[:, :], mask_col).then_inc(s_mask_col, 16)
            act.dma_start(mrow8[:, :], mask_row.broadcast_to([P, TOKENS])).then_inc(s_mask_row, 16)
            act.dma_start(w_att_sb[:, :], w_att).then_inc(s_wproj, 16)
            act.dma_start(bias_sb[:, :], router_bias.broadcast_to([P, EXPERTS])).then_inc(s_wproj, 16)

            def mask_row_of(g):
                nc.scalar.copy(mix_all[:, g * GT:(g + 1) * GT, :].rearrange("p t k -> p (t k)"),
                               mrow8[:, g * GN:(g + 1) * GN]).then_inc(s_mrow, 1)

            act.wait_ge(s_mask_row, 16)
            mask_row_of(0)
            act.wait_ge(s_vcol, 1)

            def mask_ctx(g):
                act.wait_ge(s_ctx[g % 2], 16 * (g // 2 + 1))
                if g >= 2:
                    act.wait_ge(s_cmix, g - 1)
                for i in range(GT):
                    last = nc.scalar.mul(ctxv_sb[g % 2][:, i, :], ctx_sb[g % 2][:, i, :],
                                         valid_col[:, g * GT + i:g * GT + i + 1])
                last.then_inc(s_ctxv, 1)

            def project(g, p):
                act.wait_ge(s_xt, g + 1)
                nc.scalar.copy(xt_sb[p][:, :], xt_ps[:, :]).then_inc(s_xt_sb, 1)
                act.wait_ge(s_cmix, g + 1)
                nc.scalar.copy(cmix_sb[p][:, :], cmix_ps[:, :]).then_inc(s_cmix_sb, 1)
                if g + 1 < GROUPS:
                    mask_ctx(g + 1)
                else:
                    peel(step, LEAD)
                act.wait_ge(s_q, g + 1)
                nc.scalar.copy(q_all[:, g * GT:(g + 1) * GT, :, :].rearrange("p t g s -> p g t s"),
                               q_ps[:, :].rearrange("p (g t s) -> p g t s", g=2, t=GT)).then_inc(s_q_sb, 1)
                act.wait_ge(s_k, g + 1)
                nc.scalar.copy(k_all[:, g * GT:(g + 1) * GT, :, :].rearrange("p t g s -> p g t s"),
                               k_ps[:, :].rearrange("p (g t s) -> p g t s", g=2, t=GT)).then_inc(s_k_sb, 1)
            mask_ctx(0)
            for g in range(1, GROUPS):
                mask_row_of(g)

            def step(t, p, on):
                q = 1 - p
                if isinstance(t, int) and t == TILES - 2:
                    tanh_of(0)
                if on(-1):
                    if isinstance(t, int) and t < 0:
                        act.wait_ge(s_vwide, 2)
                        act.wait_ge(s_vden, 2)
                        act.wait_ge(s_v_sb, 1)
                    elif isinstance(t, int) and t == 0:
                        act.wait_ge(s_v_sb, GROUPS)
                    nc.scalar.copy(v_blk[q][:, :, :, 0:2 * DV].rearrange("p b j w -> p (b j) w"),
                                   v_all[:, bass.ds(t + 1, 1), :, :, :, :].rearrange("p o b j e d -> p (o b j) (e d)"))\
                        .then_inc(s_vblk, 1)
                if on(0):
                    cols = bass.ds(t * W_STEP, W_STEP)
                    nc.scalar.copy(w_hi[:, cols], w_moe_sb[:, cols]).then_inc(s_w_hi, 1)

                def transposed(h):
                    act.wait_ge(s_pt[h], t + 1)
                    nc.scalar.copy(prob_t[p][:, h * GT:(h + 1) * GT, :],
                                   pt_ps[h][:, :].rearrange("p (j q) -> p j q", q=P)).then_inc(s_pt_sb[h], 1)

                def exponentials(g):
                    act.wait_ge(s_sub[g], t + 2)
                    nc.scalar.activation(prob[q][:, g * GN:(g + 1) * GN], prob[q][:, g * GN:(g + 1) * GN], ACT.Exp,
                                         scale=SCORE_SCALE).then_inc(s_exp[g], 1)

                if on(0):
                    transposed(0)
                if on(2):
                    act.wait_ge(s_bias2, t - 1)
                    nc.scalar.activation(xn2[p][:, :], x_sb[:, bass.ds(t - 2, 1), :].rearrange("p o d -> p (o d)"),
                                         ACT.Identity, scale=rstd2[p][:, :], bias=bias2[p][:, :]).then_inc(s_xn2, 1)
                if on(1):
                    act.wait_ge(s_at, t)
                    nc.scalar.copy(att_t[q][:, :], at_ps[:, 0:P]).then_inc(s_at_sb, 1)
                if on(0):
                    transposed(1)
                if on(2):
                    act.wait_ge(s_xt2, t - 1)
                    cols = bass.ds((t - 2) * P, P)
                    nc.scalar.copy(xt2[p][:, :], tail_ps[:, 0:P])
                    nc.scalar.copy(xt2_hi[:, cols], tail_ps[:, 0:P]).then_inc(s_xt2_hi, 1)
                if on(-1):
                    exponentials(0)
                if on(0):
                    act.wait_ge(s_pvt, t + 1)
                    nc.scalar.copy(pvt_sb[:, :], pvt_ps).then_inc(s_pvt_sb, 1)
                if on(-1):
                    exponentials(1)

            def tanh_of(half):
                tiles = slice(half * TILES // 2, (half + 1) * TILES // 2)
                act.wait_ge(s_top_f, (half + 1) * TILES // 2)
                nc.scalar.activation(half_tanh[:, tiles], gap[:, tiles], ACT.Tanh, scale=0.5).then_inc(s_tanh, 1)

            for g in range(GROUPS):
                project(g, g % 2)
            def slot(g, m):
                n, r = g * UNITS + m, m % 2
                if m == 2 and exists(g, m, back=UNITS):
                    act.wait_ge(s_down, g * UNITS)
                    nc.scalar.copy(moe_t[:, :], moe_ps[:, :]).then_inc(s_moe_sb, 1)
                if exists(g, m):
                    act.wait_ge(s_gate, n + 1)
                    if exists(g, m, back=2):
                        act.wait_ge(s_hid_u, n - back_to_buffer(m) + 1)
                    nc.scalar.activation(sig[r][:, :], gate_ps[r][:, :], ACT.Silu).then_inc(s_sig, 1)
                if isinstance(g, int) and (g, m) == (0, 1):
                    act.wait_ge(s_ct, 1)
                    nc.scalar.copy(comb_t[:, 0:2 * GN], bank_bf16(cb_ps[0])[0:PARTS * EXPERTS, 0:2 * GN])\
                        .then_inc(s_ct_sb, 1)
                if exists(g, m, back=1):
                    k = (m - 1) % 3
                    wait_hid(act, g, m - 1)
                    if exists(g, m, back=4):
                        act.wait_ge(s_down, n - 3)
                    nc.scalar.copy(hid_hi[k][:, :], hid[k][:, :]).then_inc(s_hid_hi, 1)
                if isinstance(g, int) and (g, m) == (0, UNITS - 1):
                    act.wait_ge(s_ct, 2)
                    nc.scalar.copy(comb_t[:, 2 * GN:4 * GN], bank_bf16(yt_ps)[0:PARTS * EXPERTS, 0:2 * GN])\
                        .then_inc(s_ct_sb, 1)

            act.wait_ge(s_wmoe, 48)
            pipeline(act, step)
            slot(0, 0)
            peel(step, TILES)
            slot(0, 1)
            slot(0, 2)
            peel(step, TILES + 1)
            slot(0, 3)
            slot(0, 4)
            tanh_of(1)
            expert_slots(act, slot, 5)
            act.wait_ge(s_down, GROUPS * UNITS)
            nc.scalar.copy(moe_t[:, :], moe_ps[:, :]).then_inc(s_moe_sb, 1)

        @block.vector
        def _(dve):
            def norm1(g, p):
                dve.wait_ge(s_x[g], 16)
                for i in range(GT):
                    nc.vector.bn_stats(stats1[p][:, i, :], x_sb[:, g * GT + i, :]).then_inc(s_stat1, 1)
                dve.wait_ge(s_stat1, (g + 1) * GT)
                for i in range(GT):
                    last = nc.vector.bn_aggr(mv1[p][:, i, :], stats1[p][:, i, :])
                last.then_inc(s_mv1, 1)

            def scale1(g, p):
                dve.wait_ge(s_mv1, g + 1)
                dve.wait_ge(s_rstd1, g + 1)
                if g >= 2:
                    dve.wait_ge(s_xt, g - 1)
                for i in range(GT):
                    last = nc.vector.tensor_scalar(xn[p][:, i, :], x_sb[:, g * GT + i, :], mv1[p][:, i, 0:1],
                                                   rstd1[p][:, i:i + 1], ALU.subtract, ALU.mult)
                last.then_inc(s_xn, 1)

            nc.vector.memset(v_all[:, 0:TILES // 2, :, :, :, :].rearrange("p t b j e d -> p (t b j e d)"), 0.0)\
                .then_inc(s_zero[0], 1)
            norm1(0, 0)
            dve.wait_ge(s_mask_col, 16)
            nc.vector.tensor_scalar(valid_key[:, :], mcol8[:, TILES:], -1.0, 1.0, ALU.mult, ALU.add).then_inc(s_valid, 1)
            nc.vector.tensor_scalar(valid_col[:, :], mcol8[:, 0:TILES], -1.0, 1.0, ALU.mult, ALU.add).then_inc(s_vcol, 1)
            dve.wait_ge(s_nvalid, 1)
            nc.vector.tensor_scalar(n_valid[:, :], count_ps[:, 0:BATCHES], 1.0, None, ALU.max).then_inc(s_cnt, 1)
            nc.vector.tensor_scalar(none_valid[:, :], count_ps[:, 0:BATCHES], 0.0, None, ALU.is_equal).then_inc(s_cnt, 1)
            dve.wait_ge(s_cnt, 2)
            nc.vector.reciprocal(inv_valid[:, :], n_valid[:, :]).then_inc(s_cnt, 1)
            nc.vector.tensor_tensor(share_key[:, :], valid_key[:, :], none_valid[:, :], ALU.add).then_inc(s_share, 1)
            dve.wait_ge(s_cnt, 3)
            dve.wait_ge(s_const, 16)
            nc.vector.tensor_tensor(
                inv_half[:, :].rearrange("p (t b) -> p t b", b=BPT), inv_valid[:, :].rearrange("p (t b) -> p t b", b=BPT),
                half_mask_sb.rearrange("p (o b) -> p o b", o=1).broadcast_to([P, TILES, BPT]), ALU.mult).then_inc(s_ihalf, 1)
            scale1(0, 0)
            dve.wait_ge(s_share, 1)
            for h in range(2):
                dve.wait_ge(s_zero[h], 1)
            for e in range(2):
                rows = slice(e * S, (e + 1) * S)
                nc.vector.tensor_copy(
                    v_all[rows, :, :, :, e, DK].rearrange("p t b j -> p (t b) j"),
                    share_key[rows, :].rearrange("p (c o) -> p c o", o=1).broadcast_to([S, BATCHES, PAIRS])).then_inc(s_vden, 1)

            def top_two(half):
                tiles = slice(half * TILES // 2, (half + 1) * TILES // 2)
                shape = [P, TILES // 2, EXPERTS]
                iota_bc = iota_sb.rearrange("p (o e) -> p o e", o=1).broadcast_to(shape)
                dve.wait_ge(s_top_f, (half + 1) * TILES // 2)
                for k, dst in ((0, comb), (1, comb_b)):
                    nc.vector.tensor_tensor(dst[:, tiles, :], iota_bc, top_f[:, tiles, k:k + 1].broadcast_to(shape),
                                            ALU.is_equal)
                dve.wait_ge(s_tanh, half + 1)
                for k, sign in ((0, -0.5), (1, 0.5)):
                    last = nc.vector.tensor_scalar(w_top[:, tiles, k], half_tanh[:, tiles], sign, 0.5, ALU.mult, ALU.add)
                last.then_inc(s_w_top, 1)

            def step(t, p, on):
                q = 1 - p
                if on(2):
                    x1 = x_sb[:, bass.ds(t - 2, 1), :].rearrange("p o d -> p (o d)")
                    dve.wait_ge(s_wo, t - 1)
                    nc.vector.tensor_tensor(x1, x1, wo_ps[:, 0:D], ALU.add).then_inc(s_x1, 1)
                if on(3):
                    dve.wait_ge(s_logit, t - 2)
                    nc.vector.tensor_tensor(logit[q][:, :], tail_ps[:, 0:EXPERTS], bias_sb[:, :],
                                            ALU.add).then_inc(s_logit_sb, 1)
                if on(2):
                    dve.wait_ge(s_x1, t - 1)
                    nc.vector.memset(pause[:, 4 + p:5 + p], 0.0)
                    nc.vector.bn_stats(stats2[p][:, :], x1).then_inc(s_stat2, 1)
                if on(3):
                    dve.wait_ge(s_logit_sb, t - 2)
                    nc.vector.memset(pause[:, q:q + 1], 0.0)
                    nc.vector.max(top_v[q][:, :], logit[q][:, :]).then_inc(s_top_v, 1)
                if on(2):
                    dve.wait_ge(s_stat2, t - 1)
                    nc.vector.memset(pause[:, 6 + p:7 + p], 0.0)
                    nc.vector.bn_aggr(mv2[p][:, :], stats2[p][:, :]).then_inc(s_mv2, 1)
                if on(3):
                    dve.wait_ge(s_top_v, t - 2)
                    nc.vector.memset(pause[:, 2 + q:3 + q], 0.0)
                    nc.vector.max_index(top_i[q][:, :], top_v[q][:, :], logit[q][:, :]).then_inc(s_top_i, 1)
                    tile = bass.ds(t - 3, 1)
                    nc.vector.tensor_tensor(gap[:, tile], top_v[q][:, 1:2], top_v[q][:, 0:1], ALU.subtract)
                if on(2):
                    dve.wait_ge(s_mv2, t - 1)
                    nc.vector.tensor_scalar(neg_mean2[p][:, :], mv2[p][:, 0:1], -1.0, None, ALU.mult).then_inc(s_nmean2, 1)
                if on(3):
                    dve.wait_ge(s_top_i, t - 2)
                    nc.vector.tensor_copy(top_f[:, tile, :].rearrange("p o k -> p (o k)"),
                                          top_i[q][:, 0:2]).then_inc(s_top_f, 1)

                def row_max(g):
                    dve.wait_ge(s_score[g], t + 2)
                    nc.vector.tensor_reduce(smax[q][:, g * HG:(g + 1) * HG],
                                            score_ps[g][:, :].rearrange("p (h s) -> p h s", s=S), AX_X,
                                            ALU.max).then_inc(s_max[g], 1)

                if on(-1):
                    row_max(0)
                if on(1):
                    pv = pv_ps.rearrange("p (j w) -> p j w", w=PW)[:, :, 0:2 * DV].rearrange("p j (e d) -> p j e d", e=2)
                    dve.wait_ge(s_pv, t)
                    nc.vector.reciprocal(inv_den[q][:, :].rearrange("p (j e) -> p j e", e=2), pv[:, :, :, DK]).then_inc(s_iden, 1)
                    dve.wait_ge(s_iden, t)
                    nc.vector.tensor_tensor(
                        att[q][:, :, :].rearrange("p (j e) d -> p j e d", e=2), pv[:, :, :, 0:DK],
                        inv_den[q][:, :].rearrange("p (j e o) -> p j e o", e=2, o=1).broadcast_to([P, PAIRS, 2, DK]),
                        ALU.mult).then_inc(s_att, 1)
                if on(-1):
                    for g in range(2):
                        if g == 1:
                            row_max(1)
                        dve.wait_ge(s_max[g], t + 2)
                        nc.vector.tensor_tensor(
                            prob[q][:, g * GN:(g + 1) * GN].rearrange("p (h s) -> p h s", s=S),
                            score_ps[g][:, :].rearrange("p (h s) -> p h s", s=S),
                            smax[q][:, g * HG:(g + 1) * HG].rearrange("p (h o) -> p h o", o=1).broadcast_to([P, HG, S]),
                            ALU.subtract).then_inc(s_sub[g], 1)
                if isinstance(t, int) and t == TILES - 1:
                    top_two(0)
                    expert_weights(dve, nc.vector, 0, s_route[0])

            for g in range(GROUPS):
                p = g % 2
                if g == GROUPS - 1:
                    peel(step, LEAD)
                if g + 1 < GROUPS:
                    norm1(g + 1, 1 - p)
                if g + 1 < GROUPS:
                    scale1(g + 1, 1 - p)
                dve.wait_ge(s_v, g + 1)
                for b in range(BPT):
                    rows = slice(b * S, (b + 1) * S)
                    share = share_key[rows, g * GT * BPT:(g + 1) * GT * BPT].rearrange("p (t b) -> p t b", b=BPT)
                    for e in range(2):
                        last = nc.vector.tensor_tensor(
                            v_all[e * S:(e + 1) * S, g * GT:(g + 1) * GT, b, :, e, 0:DK],
                            v_ps[rows, :].rearrange("p (t j e d) -> p t j e d", t=GT, e=2, d=DK)[:, :, :, e, :],
                            share[:, :, b].rearrange("p (t j d) -> p t j d", j=1, d=1).broadcast_to([S, GT, PAIRS, DK]),
                            ALU.mult)
                last.then_inc(s_v_sb, 1)

            dve.wait_ge(s_wproj, 32)
            def result(g):
                rows = x_sb[:, bass.ds(g * GT, GT), :]
                dve.wait_ge(s_yt, g + 1)
                nc.vector.tensor_tensor(rows, yt_ps[:, :].rearrange("p (t d) -> p t d", d=D), rows,
                                        ALU.add).then_inc(s_y, 1)

            def slot(g, m):
                n, r, k = g * UNITS + m, m % 2, m % 3
                if exists(g, m):
                    dve.wait_ge(s_sig, n + 1)
                    dve.wait_ge(s_up, n + 1)
                    dst = hid_u[r] if m > 0 else hid[k]
                    nc.vector.tensor_tensor(dst[:, :], sig[r][:, :], up_ps[r][:, :], ALU.mult).then_inc(s_hid_u, 1)
                if exists(g, m, back=1):
                    kb = (m - 1) % 3
                    dve.wait_ge(s_hid_hi, n)
                    if exists(g, m, back=4):
                        dve.wait_ge(s_down, n - 3)
                    nc.vector.tensor_tensor(hid_lo[kb][:, :], hid[kb][:, :], hid_hi[kb][:, :].bitcast(F32),
                                            ALU.subtract).then_inc(s_hid_lo, 1)
                if exists(g, m) and m > 0:
                    dve.wait_ge(s_hid_u, n + 1)
                    dve.wait_ge(s_cb, g * EPAIRS + m)
                    nc.vector.tensor_tensor(hid[k][:, :], hid_u[r][:, :], cb_ps[r][:, :], ALU.mult).then_inc(s_hid, 1)
                if m == 3 and exists(g, m, back=UNITS):
                    result(g - 1)

            pipeline(dve, step)
            peel(step, TILES)
            slot(0, 0)
            slot(0, 1)
            peel(step, TILES + 1)
            slot(0, 2)
            slot(0, 3)
            peel(step, TILES + 2)
            slot(0, 4)
            slot(0, 5)
            top_two(1)
            expert_slots(dve, slot, 6)
            result(GROUPS - 1)

        @block.tensor
        def _(pe):
            def keep_busy(products):
                for _ in range(products):
                    nc.tensor.matmul(score_ps[0][:, 0:P], half_sb[:, :], half_sb[:, :], start=True, stop=True)

            pe.wait_ge(s_half, 1)
            keep_busy(8)
            pe.wait_ge(s_valid, 1)
            nc.tensor.matmul(count_ps[:, 0:BATCHES], half_sb[:, :], valid_key[:, :], start=True,
                             stop=True).then_inc(s_nvalid, 1)
            keep_busy(6)
            pe.wait_ge(s_const, 16)

            def project(g, p, first=False):
                pe.wait_ge(s_xn, g + 1)
                if not first:
                    pe.wait_ge(s_xt_sb, g)
                for i in range(GT):
                    last = nc.tensor.transpose(xt_ps[:, i * P:(i + 1) * P], xn[p][:, i, :], ident_sb)
                last.then_inc(s_xt, 1)
                if first:
                    pe.wait_ge(s_wproj, 32)
                pe.wait_ge(s_ctxt[p], 16 * (g // 2 + 1))
                if not first:
                    pe.wait_ge(s_v_sb, g)
                for i in range(GT):
                    last = nc.tensor.matmul(v_ps[:, i * P:(i + 1) * P], ctxt_sb[p][:, i * P:(i + 1) * P], wv_sb,
                                            start=True, stop=True)
                last.then_inc(s_v, 1)
                pe.wait_ge(s_ctxv, g + 1)
                pe.wait_ge(s_mix, g + 1)
                if not first:
                    pe.wait_ge(s_cmix_sb, g)
                for i in range(GT):
                    last = nc.tensor.matmul(cmix_ps[:, i * P:(i + 1) * P], ctxv_sb[p][:, i, :], mix_all[:, g * GT + i, :],
                                            start=True, stop=True)
                last.then_inc(s_cmix, 1)
                for w, src, have, dst, drained, made in ((wq_sb, xt_sb, s_xt_sb, q_ps, s_q_sb, s_q),
                                                        (wk_sb, cmix_sb, s_cmix_sb, k_ps, s_k_sb, s_k)):
                    pe.wait_ge(have, g + 1)
                    if not first:
                        pe.wait_ge(drained, g)
                    for hg in range(2):
                        for b in range(BPT):
                            last = nc.tensor.matmul(
                                dst[b * ROWS:(b + 1) * ROWS, hg * GT * S:(hg + 1) * GT * S],
                                w[:, hg * ROWS:(hg + 1) * ROWS],
                                src[p][:, :].rearrange("p (t b s) -> p t b s", b=BPT, s=S)[:, :, b, :],
                                start=True, stop=True)
                    last.then_inc(made, 1)

            def values_as_rows(t):
                pe.wait_ge(s_pvt_sb, t + 1)
                for g in range(2):
                    last = nc.tensor.transpose(pv_ps[:, g * P:(g + 1) * P], pvt_sb[:, g * P:(g + 1) * P], ident_sb)
                last.then_inc(s_pv, 1)

            def attention_transposed(t, p):
                pe.wait_ge(s_att, t + 1)
                nc.tensor.transpose(at_ps, att[p][:, :, :].rearrange("p h d -> p (h d)"), ident_sb).then_inc(s_at, 1)

            def output_projection(t, p):
                pe.wait_ge(s_at_sb, t + 1)
                nc.tensor.matmul(wo_ps, att_t[p][:, :], wo_sb, start=True, stop=True).then_inc(s_wo, 1)

            def norm_transposed(t, p):
                pe.wait_ge(s_xn2, t + 1)
                if not (isinstance(t, int) and t < 1):
                    pe.wait_ge(s_logit_sb, t)
                nc.tensor.transpose(tail_ps, xn2[p][:, :], ident_sb).then_inc(s_xt2, 1)

            def router(t, p):
                pe.wait_ge(s_xt2_hi, t + 1)
                nc.tensor.matmul(tail_ps[:, 0:EXPERTS], xt2[p][:, :], wr_sb, start=True, stop=True).then_inc(s_logit, 1)

            def step(t, p, on):
                q = 1 - p
                once = isinstance(t, int)

                def transposes(h):
                    pe.wait_ge(s_exp[h], t + 1)
                    for j in range(GT):
                        c = (h * GT + j) * P
                        last = nc.tensor.transpose(pt_ps[h][:, j * P:(j + 1) * P], prob[p][:, c:c + P], ident_sb)
                    last.then_inc(s_pt[h], 1)

                def values(h):
                    pe.wait_ge(s_pt_sb[h], t + 1)
                    for c in range(GT):
                        j = h * GT + c
                        for b in range(BPT):
                            last = nc.tensor.matmul(
                                pvt_ps[c * PW:(c + 1) * PW, h * P + b * S:h * P + (b + 1) * S], v_blk[p][:, b, j, :],
                                prob_t[p][:, j, b * S:(b + 1) * S], start=True, stop=True, tile_position=(0, c * PW))
                    return last

                def scores(g):
                    if not (once and t < 0):
                        pe.wait_ge(s_sub[g], t + 1)
                    nc.tensor.matmul(score_ps[g][:, :], q_blk[q][:, g, :, :].rearrange("p b s -> p (b s)"),
                                     k_blk[q][:, g, :, :].rearrange("p h s -> p (h s)"), start=True,
                                     stop=True).then_inc(s_score[g], 1)

                if on(-1):
                    pe.wait_ge(s_blk, t + 2)
                    scores(0)
                if on(1):
                    if once and t == 1:
                        pe.wait_ge(s_v_sb, GROUPS)
                    values_as_rows(t - 1)
                if on(0):
                    transposes(0)
                if on(-1):
                    scores(1)
                if on(1):
                    attention_transposed(t - 1, q)
                if on(0):
                    transposes(1)
                if on(2):
                    norm_transposed(t - 2, p)
                if on(0):
                    pe.wait_ge(s_vblk, t + 1)
                    values(0)
                if on(1):
                    output_projection(t - 1, q)
                if on(0):
                    values(1).then_inc(s_pvt, 1)
                if on(2):
                    router(t - 2, p)

            for g in range(GROUPS):
                if g == GROUPS - 1:
                    peel(step, LEAD)
                project(g, g % 2, first=g == 0)
            def three_products(out, w_parts, moving_parts, start, stop):
                (wh, wl), (mh, ml) = w_parts, moving_parts
                for k, (w, moving) in enumerate(((wh, mh), (wh, ml), (wl, mh))):
                    last = nc.tensor.matmul(out, w, moving, start=start and k == 0, stop=stop and k == 2)
                return last

            def sums_as_rows():
                for k in range(GT):
                    last = nc.tensor.transpose(yt_ps[:, k * P:(k + 1) * P], moe_t[:, k * P:(k + 1) * P], ident_sb)
                last.then_inc(s_yt, 1)

            def weights_as_rows(half, bank):
                pe.wait_ge(s_comb3, half + 1)
                for k in range(2 * GT):
                    last = nc.tensor.transpose(bank_bf16(bank)[0:PARTS * EXPERTS, k * P:(k + 1) * P],
                                               comb3[:, k, :, :].rearrange("p k e -> p (k e)"), identb_sb[:, :])
                last.then_inc(s_ct, 1)

            def gate(g, m):
                n, r = g * UNITS + m, m % 2
                if m == 0:
                    pe.wait_ge(s_xt2_lo, g * GT + GT)
                if isinstance(g, int):
                    pe.wait_ge(s_w_lo, m + 1)
                if exists(g, m, back=2):
                    pe.wait_ge(s_sig, n - back_to_buffer(m) + 1)
                three_products(gate_ps[r][:, :], (w_slice(w_hi, m, 0), w_slice(w_lo, m, 0)), x_parts(g),
                               True, True).then_inc(s_gate, 1)

            def up(g, m):
                n, r = g * UNITS + m, m % 2
                if exists(g, m, back=2):
                    pe.wait_ge(s_hid_u, n - back_to_buffer(m) + 1)
                if m >= 3:
                    wait_hid(pe, g, m - 2)
                elif m > 0 and not isinstance(g, int):
                    wait_hid(pe, g, m - 3)
                three_products(up_ps[r][:, :], (w_slice(w_hi, m, 1), w_slice(w_lo, m, 1)), x_parts(g),
                               True, True).then_inc(s_up, 1)

            def token_weights(g, m):
                pe.wait_ge(s_ct_sb, 1 if isinstance(g, int) else 2)
                nc.tensor.matmul(cb_ps[m % 2][:, :], sel_sb[:, m - 1, :], comb_t[:, bass.ds(g * GN, GN)], start=True,
                                 stop=True).then_inc(s_cb, 1)

            def x_parts(g):
                return xt2_hi[:, bass.ds(g * GN, GN)], xt2_lo[:, bass.ds(g * GN, GN)]

            def slot(g, m):
                n = g * UNITS + m
                if exists(g, m):
                    gate(g, m)
                    if isinstance(g, int) and m == UNITS - 1:
                        weights_as_rows(1, yt_ps)
                    up(g, m)
                    if m > 0:
                        token_weights(g, m)
                if exists(g, m, back=2):
                    u = (m - 2) % UNITS
                    if u == 0 and exists(g, m, back=UNITS):
                        pe.wait_ge(s_moe_sb, g)
                    pe.wait_ge(s_hid_lo, n - 1)
                    three_products(moe_ps[:, :], (w_slice(w_hi, u, 2), w_slice(w_lo, u, 2)),
                                   (hid_hi[u % 3][:, :], hid_lo[u % 3][:, :]), u == 0, u == UNITS - 1).then_inc(s_down, 1)
                    if u == 0 and exists(g, m, back=UNITS):
                        sums_as_rows()

            pipeline(pe, step)
            gate(0, 0)
            values_as_rows(TILES - 1)
            up(0, 0)
            attention_transposed(TILES - 1, 1)
            gate(0, 1)
            weights_as_rows(0, cb_ps[0])
            norm_transposed(TILES - 2, 0)
            output_projection(TILES - 1, 1)
            up(0, 1)
            router(TILES - 2, 0)
            token_weights(0, 1)
            pe.wait_ge(s_x1, TILES)
            slot(0, 2)
            norm_transposed(TILES - 1, 1)
            slot(0, 3)
            router(TILES - 1, 1)
            expert_slots(pe, slot, 4)
            pe.wait_ge(s_moe_sb, GROUPS)
            sums_as_rows()


def host_layout(inputs):
    a = {k: np.asarray(v) for k, v in inputs.items()}
    c = np.ascontiguousarray
    mask = a["mask_Bx1x1xS2_bk0"].reshape(TOKENS)
    key_rows = mask.reshape(BATCHES, S).T
    ctx = a["ctx_1024"].reshape(TOKENS, D)

    def pairs(w):
        return w.transpose(1, 0, 2).reshape(D, EPAIRS, P)

    gate = np.concatenate([a["L0_ffn_sh_gate"].T[:, None, :], pairs(a["L0_ffn_gate_proj"])], axis=1)
    up = np.concatenate([a["L0_ffn_sh_up"].T[:, None, :], pairs(a["L0_ffn_up_proj"])], axis=1)
    down = np.concatenate([a["L0_ffn_sh_down"].T[:, None, :],
                           a["L0_ffn_down_proj"].reshape(EPAIRS, P, D).transpose(1, 0, 2)], axis=1)
    w_moe = np.stack([gate, up, down], axis=2).reshape(P, W_MOE)
    w_att = np.concatenate([a["L0_xattn_" + w].T for w in ("Wq", "Wk", "Wv", "Wo")] + [a["L0_ffn_router_w"].T], axis=1)
    ident = np.eye(P, dtype=np.float32)
    head_of_row = (np.arange(P) % ROWS) // DK
    head_mask = (head_of_row[:, None] == np.arange(HG)[None, :]).astype(np.float32)
    expert_of_row = np.arange(PARTS * EXPERTS) % EXPERTS
    expert_of_col = (2 * np.arange(EPAIRS)[:, None] + np.arange(P)[None, :] // E_DIM)
    sel = expert_of_row[:, None, None] == expert_of_col[None]
    bf16 = mybir.dt.np(BF16)
    half_mask = (np.arange(P)[:, None] // S == np.arange(2)[None, :]).astype(np.float32)
    iota = np.tile(np.arange(EXPERTS, dtype=np.float32), (P, 1))
    return {
        "x": c(a["x"].reshape(TOKENS, D)), "ctx_nat": c(ctx), "ctx_t": c(ctx.T),
        "mask_row": c(mask.reshape(1, TOKENS)),
        "mask_col": c(np.concatenate([mask.reshape(TILES, P).T, np.concatenate([key_rows, key_rows], axis=0)], axis=1)),
        "w_att": c(w_att), "router_bias": c(a["L0_ffn_router_bias"].reshape(1, EXPERTS)), "w_moe": c(w_moe),
        "consts": c(np.concatenate([ident, head_mask, half_mask, iota], axis=1)),
        "ident_bf": ident.astype(bf16), "expert_sel": sel.astype(bf16),
    }


def kernel(**inputs):
    import concourse.bacc as bacc
    from concourse.bass_utils import run_bass_kernel_spmd

    nc = bacc.Bacc("TRN2", target_bir_lowering=False, num_devices=1)
    arrays = host_layout(inputs)
    args = {n: nc.dram_tensor(n, a.shape, mybir.dt.from_np(a.dtype), kind="ExternalInput").ap()
            for n, a in arrays.items()}
    out = nc.dram_tensor("out", (TOKENS, D), F32, kind="ExternalOutput").ap()
    build_program(nc, out=out, **args)
    r = run_bass_kernel_spmd(nc, [arrays], core_ids=[0])
    return r.results[0]["out"].reshape(BATCHES, S, D)
```
